# Optimizing a Trainium2 kernel written in Bass

```python
import numpy as np
import jax
import jax.numpy as jnp

def _softmax(x, axis=-1):
    return jax.nn.softmax(x, axis=axis)

def _gelu(x):
    return jax.nn.gelu(x, approximate=True)

def _silu(x):
    return jax.nn.silu(x)

def _sigmoid(x):
    return jax.nn.sigmoid(x)

def _layernorm(x, axis=-1, eps=1e-05):
    m = jnp.mean(x, axis=axis, keepdims=True)
    v = jnp.var(x, axis=axis, keepdims=True)
    return (x - m) / jnp.sqrt(v + eps)

def _scatter_add(tgt, idx, src, axis=0):
    return tgt.at[idx].add(src)

def _segment_sum(src, seg, n):
    return jax.ops.segment_sum(src, seg, n)
kernel_name = 'mk_adj_preln_d4_adj_r2_bbeea8'

def setup_inputs(seed: int=0):
    np.random.seed(seed)
    _w = jnp.asarray

    def _rec_inputs():
        import jax
        import jax.numpy as jnp
        _gk = jax.random.key(seed)
        x = -0.0001538 + 1 * jax.random.normal(jax.random.fold_in(_gk, 1), (64, 128, 384), jnp.float32)
        _w = (1.0 + jnp.arange(128, dtype=jnp.float32)) ** (-0.5)
        _w = _w / _w.mean()
        _pij = jnp.clip(0.125 * _w[:, None] * _w[None, :], 0.0, 1.0)
        _a = jax.random.uniform(jax.random.fold_in(_gk, 2), (64, 128, 128)) < _pij
        _a = jnp.logical_or(_a, jnp.eye(128, dtype=bool))
        adj = _a
        return (x, adj)
    x, adj = _rec_inputs()

    def _L0_gnn_setup():
        import jax, jax.numpy as jnp
        import numpy as np
        B, S, H = (4, 1024, 384)
        NUM_HEADS = 6
        HEAD_SIZE = H // NUM_HEADS
        NEG = -9000000000000000.0

        def _heads(x):
            b, s, _ = x.shape
            return x.reshape(b, s, NUM_HEADS, HEAD_SIZE).transpose(0, 2, 1, 3)
        key = jax.random.key(seed)
        ks = jax.random.split(key, 10)
        seq_inputs = jax.random.normal(ks[0], (B, S, H), dtype=jnp.float32)
        gm = jax.random.randint(ks[1], (B, S, S), 0, 2) > 0
        graph_mask = gm | jnp.eye(S, dtype=bool)[None]
        sc = 1.0 / np.sqrt(H)
        Wq = jax.random.normal(ks[2], (H, H), dtype=jnp.float32) * sc
        bq = jnp.zeros((H,), dtype=jnp.float32)
        Wk = jax.random.normal(ks[3], (H, H), dtype=jnp.float32) * sc
        bk = jnp.zeros((H,), dtype=jnp.float32)
        Wv = jax.random.normal(ks[4], (H, H), dtype=jnp.float32) * sc
        bv = jnp.zeros((H,), dtype=jnp.float32)
        Wf = jax.random.normal(ks[5], (H, H), dtype=jnp.float32) * sc
        bf = jnp.zeros((H,), dtype=jnp.float32)
        return {'seq_inputs': seq_inputs, 'Wq': Wq, 'bq': bq, 'Wk': Wk, 'bk': bk, 'Wv': Wv, 'bv': bv, 'Wf': Wf, 'bf': bf, 'graph_mask': graph_mask}
    _L0_gnn_all = _L0_gnn_setup()
    _L0_gnn_in = {k: v for k, v in _L0_gnn_all.items() if k in ('Wq', 'bq', 'Wk', 'bk', 'Wv', 'bv', 'Wf', 'bf')}
    del _L0_gnn_all

    def _L1_gnn_setup():
        import jax, jax.numpy as jnp
        import numpy as np
        ATT_HEAD = 12
        IN_DIM = 384
        OUT_DIM = IN_DIM // ATT_HEAD
        LEAKY_ALPHA = 0.2
        B, N = (8, 256)
        key = jax.random.key(seed)
        ks = jax.random.split(key, 8)
        feat_in = jax.random.normal(ks[0], (B, N, IN_DIM), dtype=jnp.float32)
        adj = jax.random.randint(ks[1], (B, N, N), 0, 2) > 0
        lim_W = float(np.sqrt(6.0 / (IN_DIM + OUT_DIM)))
        W = jax.random.uniform(ks[2], (ATT_HEAD, IN_DIM, OUT_DIM), minval=-lim_W, maxval=lim_W, dtype=jnp.float32)
        b = jnp.zeros((OUT_DIM,), dtype=jnp.float32)
        lim_w = float(np.sqrt(6.0 / (OUT_DIM + 1)))
        w_src = jax.random.uniform(ks[3], (ATT_HEAD, OUT_DIM, 1), minval=-lim_w, maxval=lim_w, dtype=jnp.float32)
        w_dst = jax.random.uniform(ks[4], (ATT_HEAD, OUT_DIM, 1), minval=-lim_w, maxval=lim_w, dtype=jnp.float32)
        std_H = float(np.sqrt(2.0 / (IN_DIM + IN_DIM)))
        H_w = jax.random.normal(ks[5], (IN_DIM, IN_DIM), dtype=jnp.float32) * std_H
        H_b = jax.random.normal(ks[6], (IN_DIM,), dtype=jnp.float32) * 0.01
        return {'feat_in': feat_in, 'adj': adj, 'W': W, 'b': b, 'w_src': w_src, 'w_dst': w_dst, 'H_w': H_w, 'H_b': H_b}
    _L1_gnn_all = _L1_gnn_setup()
    _L1_gnn_in = {k: v for k, v in _L1_gnn_all.items() if k in ('W', 'b', 'w_src', 'w_dst', 'H_w', 'H_b')}
    del _L1_gnn_all

    def _L2_gnn_setup():
        import jax, jax.numpy as jnp
        import numpy as np
        B, S, H = (4, 1024, 384)
        NUM_HEADS = 6
        HEAD_SIZE = H // NUM_HEADS
        NEG = -9000000000000000.0

        def _heads(x):
            b, s, _ = x.shape
            return x.reshape(b, s, NUM_HEADS, HEAD_SIZE).transpose(0, 2, 1, 3)
        key = jax.random.key(seed)
        ks = jax.random.split(key, 10)
        seq_inputs = jax.random.normal(ks[0], (B, S, H), dtype=jnp.float32)
        gm = jax.random.randint(ks[1], (B, S, S), 0, 2) > 0
        graph_mask = gm | jnp.eye(S, dtype=bool)[None]
        sc = 1.0 / np.sqrt(H)
        Wq = jax.random.normal(ks[2], (H, H), dtype=jnp.float32) * sc
        bq = jnp.zeros((H,), dtype=jnp.float32)
        Wk = jax.random.normal(ks[3], (H, H), dtype=jnp.float32) * sc
        bk = jnp.zeros((H,), dtype=jnp.float32)
        Wv = jax.random.normal(ks[4], (H, H), dtype=jnp.float32) * sc
        bv = jnp.zeros((H,), dtype=jnp.float32)
        Wf = jax.random.normal(ks[5], (H, H), dtype=jnp.float32) * sc
        bf = jnp.zeros((H,), dtype=jnp.float32)
        return {'seq_inputs': seq_inputs, 'Wq': Wq, 'bq': bq, 'Wk': Wk, 'bk': bk, 'Wv': Wv, 'bv': bv, 'Wf': Wf, 'bf': bf, 'graph_mask': graph_mask}
    _L2_gnn_all = _L2_gnn_setup()
    _L2_gnn_in = {k: v for k, v in _L2_gnn_all.items() if k in ('Wq', 'bq', 'Wk', 'bk', 'Wv', 'bv', 'Wf', 'bf')}
    del _L2_gnn_all

    def _L3_gnn_setup():
        import jax, jax.numpy as jnp
        import numpy as np
        ATT_HEAD = 12
        IN_DIM = 384
        OUT_DIM = IN_DIM // ATT_HEAD
        LEAKY_ALPHA = 0.2
        B, N = (8, 256)
        key = jax.random.key(seed)
        ks = jax.random.split(key, 8)
        feat_in = jax.random.normal(ks[0], (B, N, IN_DIM), dtype=jnp.float32)
        adj = jax.random.randint(ks[1], (B, N, N), 0, 2) > 0
        lim_W = float(np.sqrt(6.0 / (IN_DIM + OUT_DIM)))
        W = jax.random.uniform(ks[2], (ATT_HEAD, IN_DIM, OUT_DIM), minval=-lim_W, maxval=lim_W, dtype=jnp.float32)
        b = jnp.zeros((OUT_DIM,), dtype=jnp.float32)
        lim_w = float(np.sqrt(6.0 / (OUT_DIM + 1)))
        w_src = jax.random.uniform(ks[3], (ATT_HEAD, OUT_DIM, 1), minval=-lim_w, maxval=lim_w, dtype=jnp.float32)
        w_dst = jax.random.uniform(ks[4], (ATT_HEAD, OUT_DIM, 1), minval=-lim_w, maxval=lim_w, dtype=jnp.float32)
        std_H = float(np.sqrt(2.0 / (IN_DIM + IN_DIM)))
        H_w = jax.random.normal(ks[5], (IN_DIM, IN_DIM), dtype=jnp.float32) * std_H
        H_b = jax.random.normal(ks[6], (IN_DIM,), dtype=jnp.float32) * 0.01
        return {'feat_in': feat_in, 'adj': adj, 'W': W, 'b': b, 'w_src': w_src, 'w_dst': w_dst, 'H_w': H_w, 'H_b': H_b}
    _L3_gnn_all = _L3_gnn_setup()
    _L3_gnn_in = {k: v for k, v in _L3_gnn_all.items() if k in ('W', 'b', 'w_src', 'w_dst', 'H_w', 'H_b')}
    del _L3_gnn_all
    return {'x': x, 'adj': adj, 'L0_gnn_Wq': _L0_gnn_in['Wq'], 'L0_gnn_bq': _L0_gnn_in['bq'], 'L0_gnn_Wk': _L0_gnn_in['Wk'], 'L0_gnn_bk': _L0_gnn_in['bk'], 'L0_gnn_Wv': _L0_gnn_in['Wv'], 'L0_gnn_bv': _L0_gnn_in['bv'], 'L0_gnn_Wf': _L0_gnn_in['Wf'], 'L0_gnn_bf': _L0_gnn_in['bf'], 'L1_gnn_W': _L1_gnn_in['W'], 'L1_gnn_b': _L1_gnn_in['b'], 'L1_gnn_w_src': _L1_gnn_in['w_src'], 'L1_gnn_w_dst': _L1_gnn_in['w_dst'], 'L1_gnn_H_w': _L1_gnn_in['H_w'], 'L1_gnn_H_b': _L1_gnn_in['H_b'], 'L2_gnn_Wq': _L2_gnn_in['Wq'], 'L2_gnn_bq': _L2_gnn_in['bq'], 'L2_gnn_Wk': _L2_gnn_in['Wk'], 'L2_gnn_bk': _L2_gnn_in['bk'], 'L2_gnn_Wv': _L2_gnn_in['Wv'], 'L2_gnn_bv': _L2_gnn_in['bv'], 'L2_gnn_Wf': _L2_gnn_in['Wf'], 'L2_gnn_bf': _L2_gnn_in['bf'], 'L3_gnn_W': _L3_gnn_in['W'], 'L3_gnn_b': _L3_gnn_in['b'], 'L3_gnn_w_src': _L3_gnn_in['w_src'], 'L3_gnn_w_dst': _L3_gnn_in['w_dst'], 'L3_gnn_H_w': _L3_gnn_in['H_w'], 'L3_gnn_H_b': _L3_gnn_in['H_b']}

def reference(x, adj, L0_gnn_Wq, L0_gnn_bq, L0_gnn_Wk, L0_gnn_bk, L0_gnn_Wv, L0_gnn_bv, L0_gnn_Wf, L0_gnn_bf, L1_gnn_W, L1_gnn_b, L1_gnn_w_src, L1_gnn_w_dst, L1_gnn_H_w, L1_gnn_H_b, L2_gnn_Wq, L2_gnn_bq, L2_gnn_Wk, L2_gnn_bk, L2_gnn_Wv, L2_gnn_bv, L2_gnn_Wf, L2_gnn_bf, L3_gnn_W, L3_gnn_b, L3_gnn_w_src, L3_gnn_w_dst, L3_gnn_H_w, L3_gnn_H_b):
    import jax
    import jax.numpy as jnp

    def _L0_gnn_ref(seq_inputs, Wq, bq, Wk, bk, Wv, bv, Wf, bf, graph_mask):
        import jax, jax.numpy as jnp
        import numpy as np
        B, S, H = (4, 1024, 384)
        NUM_HEADS = 6
        HEAD_SIZE = H // NUM_HEADS
        NEG = -9000000000000000.0

        def _heads(x):
            b, s, _ = x.shape
            return x.reshape(b, s, NUM_HEADS, HEAD_SIZE).transpose(0, 2, 1, 3)
        q = _heads(seq_inputs @ Wq + bq)
        k = _heads(seq_inputs @ Wk + bk)
        v = _heads(seq_inputs @ Wv + bv)
        scores = jnp.einsum('bhqd,bhkd->bhqk', q, k) / np.sqrt(HEAD_SIZE)
        bias = jnp.where(graph_mask, 0.0, NEG)[:, None]
        probs = jax.nn.softmax(scores + bias, axis=-1)
        ctx = jnp.einsum('bhqk,bhkd->bhqd', probs, v)
        ctx = ctx.transpose(0, 2, 1, 3).reshape(seq_inputs.shape[0], seq_inputs.shape[1], H)
        return ctx @ Wf + bf

    def _L1_gnn_ref(feat_in, adj, W, b, w_src, w_dst, H_w, H_b):
        import jax, jax.numpy as jnp
        import numpy as np
        ATT_HEAD = 12
        IN_DIM = 384
        OUT_DIM = IN_DIM // ATT_HEAD
        LEAKY_ALPHA = 0.2
        B, N = (8, 256)
        h = jnp.einsum('bnd,ade->bane', feat_in, W)
        th = jnp.tanh(h)
        attn_src = jnp.einsum('bane,aeo->bano', th, w_src)
        attn_dst = jnp.einsum('bane,aeo->bano', th, w_dst)
        attn = attn_src + jnp.swapaxes(attn_dst, 2, 3)
        attn = jnp.where(attn >= 0, attn, LEAKY_ALPHA * attn)
        mask = ~adj[:, None, :, :]
        attn = jnp.where(mask, jnp.float32(-999.0), attn)
        attn = jax.nn.softmax(attn, axis=-1)
        feat_out = jnp.einsum('banm,bame->bane', attn, h) + b
        feat_out = jnp.swapaxes(feat_out, 1, 2).reshape(feat_in.shape[0], feat_in.shape[1], -1)
        feat_out = jax.nn.elu(feat_out)
        gate = jax.nn.sigmoid(feat_in @ H_w.T + H_b)
        return gate * feat_out + (1.0 - gate) * feat_in

    def _L2_gnn_ref(seq_inputs, Wq, bq, Wk, bk, Wv, bv, Wf, bf, graph_mask):
        import jax, jax.numpy as jnp
        import numpy as np
        B, S, H = (4, 1024, 384)
        NUM_HEADS = 6
        HEAD_SIZE = H // NUM_HEADS
        NEG = -9000000000000000.0

        def _heads(x):
            b, s, _ = x.shape
            return x.reshape(b, s, NUM_HEADS, HEAD_SIZE).transpose(0, 2, 1, 3)
        q = _heads(seq_inputs @ Wq + bq)
        k = _heads(seq_inputs @ Wk + bk)
        v = _heads(seq_inputs @ Wv + bv)
        scores = jnp.einsum('bhqd,bhkd->bhqk', q, k) / np.sqrt(HEAD_SIZE)
        bias = jnp.where(graph_mask, 0.0, NEG)[:, None]
        probs = jax.nn.softmax(scores + bias, axis=-1)
        ctx = jnp.einsum('bhqk,bhkd->bhqd', probs, v)
        ctx = ctx.transpose(0, 2, 1, 3).reshape(seq_inputs.shape[0], seq_inputs.shape[1], H)
        return ctx @ Wf + bf

    def _L3_gnn_ref(feat_in, adj, W, b, w_src, w_dst, H_w, H_b):
        import jax, jax.numpy as jnp
        import numpy as np
        ATT_HEAD = 12
        IN_DIM = 384
        OUT_DIM = IN_DIM // ATT_HEAD
        LEAKY_ALPHA = 0.2
        B, N = (8, 256)
        h = jnp.einsum('bnd,ade->bane', feat_in, W)
        th = jnp.tanh(h)
        attn_src = jnp.einsum('bane,aeo->bano', th, w_src)
        attn_dst = jnp.einsum('bane,aeo->bano', th, w_dst)
        attn = attn_src + jnp.swapaxes(attn_dst, 2, 3)
        attn = jnp.where(attn >= 0, attn, LEAKY_ALPHA * attn)
        mask = ~adj[:, None, :, :]
        attn = jnp.where(mask, jnp.float32(-999.0), attn)
        attn = jax.nn.softmax(attn, axis=-1)
        feat_out = jnp.einsum('banm,bame->bane', attn, h) + b
        feat_out = jnp.swapaxes(feat_out, 1, 2).reshape(feat_in.shape[0], feat_in.shape[1], -1)
        feat_out = jax.nn.elu(feat_out)
        gate = jax.nn.sigmoid(feat_in @ H_w.T + H_b)
        return gate * feat_out + (1.0 - gate) * feat_in
    h = jnp.maximum(_layernorm(x, axis=-1), 0.0)
    x = x + _L0_gnn_ref(h, L0_gnn_Wq, L0_gnn_bq, L0_gnn_Wk, L0_gnn_bk, L0_gnn_Wv, L0_gnn_bv, L0_gnn_Wf, L0_gnn_bf, adj)
    h = jnp.maximum(_layernorm(x, axis=-1), 0.0)
    x = x + _L1_gnn_ref(h, adj, L1_gnn_W, L1_gnn_b, L1_gnn_w_src, L1_gnn_w_dst, L1_gnn_H_w, L1_gnn_H_b)
    h = jnp.maximum(_layernorm(x, axis=-1), 0.0)
    x = x + _L2_gnn_ref(h, L2_gnn_Wq, L2_gnn_bq, L2_gnn_Wk, L2_gnn_bk, L2_gnn_Wv, L2_gnn_bv, L2_gnn_Wf, L2_gnn_bf, adj)
    h = jnp.maximum(_layernorm(x, axis=-1), 0.0)
    x = x + _L3_gnn_ref(h, adj, L3_gnn_W, L3_gnn_b, L3_gnn_w_src, L3_gnn_w_dst, L3_gnn_H_w, L3_gnn_H_b)
    return x

_drawn_inputs = setup_inputs


def setup_inputs(seed=0):
    import zlib

    import numpy as np

    out = dict(_drawn_inputs(seed))
    spreads = {'L0_gnn_bq': (0.0, 0.8),
     'L0_gnn_bk': (0.0, 2.0),
     'L0_gnn_bv': (0.0, 0.1),
     'L0_gnn_bf': (0.0, 0.1),
     'L1_gnn_b': (0.0, 0.28),
     'L2_gnn_bq': (0.0, 0.8),
     'L2_gnn_bk': (0.0, 2.0),
     'L2_gnn_bv': (0.0, 0.1),
     'L2_gnn_bf': (0.0, 0.1),
     'L3_gnn_b': (0.0, 0.438)}
    factors = {'L1_gnn_w_src': 27.407,
     'L1_gnn_H_b': 40.438,
     'L3_gnn_w_src': 8.0,
     'L3_gnn_w_dst': 2.757,
     'L3_gnn_H_b': 54.801}
    for name, (base, spread) in spreads.items():
        noise = np.random.default_rng([zlib.crc32(name.encode()), seed]).standard_normal(out[name].shape)
        drawn = base * np.exp(spread * noise) if base else spread * noise
        out[name] = jnp.asarray(drawn.astype(out[name].dtype))
    for name, factor in factors.items():
        out[name] = (out[name] * factor).astype(out[name].dtype)
    return out
```

```python
from contextlib import ExitStack

import concourse.bass as bass
from concourse import mybir

F32 = mybir.dt.float32
F32R = mybir.dt.float32r
BF16 = mybir.dt.bfloat16
U8 = mybir.dt.uint8
ALU = mybir.AluOpType
ACT = mybir.ActivationFunctionType
AX = mybir.AxisListType

GROUP = 4
PAIRS = 2
N = 128
D = 384
KC = D // 128
MH, MD = 6, 64
GH, GD = 12, 32
NEG = -9000000000000000.0
NO_EDGE = -999.0
SLOPE = 0.2
FAR = float(2.0**126)
LEAST = -3.0e38
EPS = 1e-5
PARTS = 3
SD = 2 * GH
LSLOTS = 3


def graph_stack(nc, x, adj, w_qk, w_vf, w_hg, b_qk, vecs, h_b, ident, sel_src, sel_dst, out):
    B = x.shape[0]
    ROUNDS = B // GROUP

    with ExitStack() as ctx:
        def sb(name, shape, dt=F32):
            return ctx.enter_context(nc.sbuf_tensor(name, shape, dt))

        def sem(name):
            return ctx.enter_context(nc.semaphore(name))

        x_mid = nc.dram_tensor("x_mid", x.shape, F32, kind="Internal").ap()

        stage = sb("stage", [128, KC, 2 * D])
        qk_hi, qk_lo = sb("qk_hi", [128, KC, 2 * D], F32R), sb("qk_lo", [128, KC, 2 * D], F32R)
        vf_hi, vf_lo = sb("vf_hi", [128, KC, 2 * D], F32R), sb("vf_lo", [128, KC, 2 * D], F32R)
        hg_hi, hg_lo = sb("hg_hi", [128, KC, 2 * D], F32R), sb("hg_lo", [128, KC, 2 * D], F32R)
        vec = sb("vec", [128, 5, D])
        bv_bc, bf_bc, bg_bc = vec[:, 0, :], vec[:, 1, :], vec[:, 2, :]
        qk_bias = sb("qk_bias", [128, 2 * KC])
        q_bias8 = sb("q_bias8", [128, KC])
        hb_row = sb("hb_row", [PARTS, D])
        hb_rest = sb("hb_rest", [PARTS, D])
        hb_part = sb("hb_part", [PARTS, PARTS, D], BF16)
        hb_acc = sb("hb_acc", [PARTS, D])
        hb3 = sb("hb3", [PARTS, D], BF16)

        idf = sb("idf", [128, 128])
        idb = sb("idb", [128, 128], BF16)
        far_id = sb("far_id", [128, 128], BF16)
        ones3 = sb("ones3", [PARTS, 128], BF16)
        sel_s = sb("sel_s", [PARTS * SD, GH, 128], BF16)
        sel_d = sb("sel_d", [PARTS * SD, GH, 128], BF16)
        minus_half = sb("minus_half", [128, 1])

        adj8 = sb("adj8", [128, GROUP, N], U8)
        neg_bias = sb("neg_bias", [128, GROUP, N])
        floor = sb("floor", [128, GROUP, N])
        no_edge = sb("no_edge", [128, GROUP, N], BF16)
        xin = sb("xin", [128, GROUP, D])
        x1 = sb("x1", [128, GROUP, D])
        hM = sb("hM", [128, GROUP, D])
        hG = sb("hG", [128, GROUP, D])
        stats = sb("stats", [128, 2, GROUP, 6])
        mv = sb("mv", [128, 2, GROUP, 2])
        var_eps = sb("var_eps", [128, 2, GROUP])
        rstd = sb("rstd", [128, 2, GROUP])
        shift = sb("shift", [128, 2, GROUP])
        hT_hi = sb("hT_hi", [128, KC, GROUP, N], F32R)
        hT_lo = sb("hT_lo", [128, KC, GROUP, N], F32R)
        big = sb("big", [128, 2 * KC * GROUP * N])
        QKT = big[:, :].rearrange("p (c n) -> p c n", c=2 * KC)
        th = big[:, 0:GROUP * D].rearrange("p (b n) -> p b n", b=GROUP)
        gate = big[:, GROUP * D:2 * GROUP * D].rearrange("p (b n) -> p b n", b=GROUP)
        vaug = sb("vaug", [128, GROUP, MH, MD + 1])
        haug = sb("haug", [128, GROUP, GH, GD + 1])
        L = sb("L", [128, LSLOTS, GH * N])
        PT = sb("PT", [128, 2, GH * N])
        mx = sb("mx", [128, 2, GH])
        rden = sb("rden", [128, 2, GH])
        ctxn = sb("ctxn", [128, 2, D])
        cT_hi = sb("cT_hi", [128, 2, KC, N], F32R)
        cT_lo = sb("cT_lo", [128, KC, N], F32R)
        prod = sb("prod", [128, 2, D])
        sd = sb("sd", [128, 2, SD])
        sd_rest = sb("sd_rest", [128, 2, 2, SD])
        sd3 = sb("sd3", [128, 2, PARTS, SD], BF16)
        sdT = sb("sdT", [PARTS * SD, 2, N], BF16)
        y = sb("y", [128, 2, D])
        ey = sb("ey", [128, 2, D])

        psum = ctx.enter_context(nc.psum_tensor("psum", [128, 8, 512], F32))
        sdT_ps = psum[0:PARTS * SD, 7, 0:N // 2].bitcast(BF16)

        def bank(i):
            return psum[:, i, :]

        def banks(i, k):
            return psum[:, i:i + k, :]

        s = {n: sem(n) for n in (
            "x_in", "adj_in", "w_in", "v_in", "const_in", "stored", "stage_split", "vecs_ready", "consts_ready",
            "setup_dve", "setup_act", "setup_pool", "hb_step", "w_ready_dve",
            "masks", "xb",
            "m_stats", "m_mv", "m_var", "m_rstd", "m_shift", "m_h", "m_hT", "m_hi", "m_lo", "m_v", "m_vaug",
            "s_ps", "s_biased", "s_max", "s_shifted", "s_exp", "pt_ps", "pt", "c_ps", "c_rden", "c_norm",
            "cT_ps", "cT_hi", "cT_lo", "o_ps", "x1",
            "g_stats", "g_mv", "g_var", "g_rstd", "g_shift", "g_h", "g_hT", "g_hi", "g_lo", "g_h_ps", "g_gate_ps",
            "g_th", "g_gate", "g_haug", "g_prod", "g_sd", "g_sd_hi", "g_rest1", "g_sd_mid", "g_rest2", "g_sd3",
            "g_sdT_ps", "g_sdT", "z_ps", "z_slope", "z_leaky", "z_masked", "z_max", "z_shifted", "z_exp", "gpt_ps", "gpt",
            "pv_ps", "pv_rden", "pv_norm", "y_min", "y_exp", "xf", "elu", "elu_f", "mixed", "x2")}
        qk_ps = [sem(f"qk_ps{c}") for c in range(2 * KC)]
        qk = [sem(f"qk{c}") for c in range(2 * KC)]

        class Round:

            def __init__(self, eng, p, g):
                t = p * ROUNDS + g
                self.k = [None] + [eng.snap(t * GROUP + k) for k in range(1, GROUP + 1)]
                self.one = eng.snap(t + 1)
                self.dma = eng.snap(t * 16 + 16)

        def done(r, b):
            return r.k[b + 1]

        def hold(eng, semaphore, value):
            eng.wait_ge(semaphore, value)
            eng.nop(nofuse=True)

        def head_of(i):
            return 2 * (i % KC) + i // KC

        block = ctx.enter_context(nc.Block())

        @block.sync
        def _(sp):
            sp.sem_inc(s["stored"], 16)
            sp.dma_start(idf[:], ident).then_inc(s["const_in"], 16)
            sp.dma_start(stage[0:PARTS * SD, 0:2, :], sel_src.rearrange("c (k n) -> c k n", k=2)).then_inc(s["const_in"], 16)
            sp.wait_ge(s["setup_dve"], 1)
            sp.dma_start(stage[0:PARTS * SD, 0:2, :], sel_dst.rearrange("c (k n) -> c k n", k=2)).then_inc(s["const_in"], 16)
            sp.wait_ge(s["setup_dve"], 2)

            def load(src, g):
                sp.dma_start(xin[:], src[bass.ds(g, GROUP), :, :].rearrange("b p n -> p b n")).then_inc(s["x_in"], 16)
                sp.dma_start(adj8[:], adj[bass.ds(g, GROUP), :, :].rearrange("b p n -> p b n")).then_inc(s["adj_in"], 16)

            def store(dst, g):
                sp.dma_start(dst[bass.ds(g, GROUP), :, :].rearrange("b p n -> p b n"), x1[:]).then_inc(s["stored"], 16)

            for pair, (src, dst) in enumerate(((x, x_mid), (x_mid, out))):
                if pair:
                    sp.wait_ge(s["x1"], ROUNDS * GROUP)
                    sp.wait_ge(s["masks"], ROUNDS)
                    sp.wait_ge(s["stored"], 16 * ROUNDS)
                load(src, 0)
                for i, w in enumerate((w_qk, w_vf, w_hg)):
                    if pair or i:
                        sp.wait_ge(s["stage_split"], 3 * pair + i)
                    sp.dma_start(stage[:], w[pair].rearrange("(c p) n -> p c n", p=128)).then_inc(s["w_in"], 16)
                if pair:
                    sp.wait_ge(s["x2"], ROUNDS * GROUP)
                    store(x_mid, (ROUNDS - 1) * GROUP)
                sp.dma_start(vec[:], vecs[pair].partition_broadcast(128)).then_inc(s["v_in"], 16)
                sp.dma_start(qk_bias[:], b_qk[pair]).then_inc(s["v_in"], 16)
                sp.dma_start(hb_row[:], h_b[pair].partition_broadcast(PARTS)).then_inc(s["v_in"], 16)
                with sp.Fori(0, ROUNDS - 1) as g:
                    here = sp.snap(g * GROUP)
                    ahead = sp.snap(g * GROUP + GROUP)
                    all_done = sp.snap(g * GROUP + (pair * ROUNDS + 1) * GROUP)
                    round_done = sp.snap(g + pair * ROUNDS + 1)
                    hold(sp, s["x1"], all_done)
                    hold(sp, s["masks"], round_done)
                    load(src, ahead)
                    hold(sp, s["x2"], all_done)
                    store(dst, here)
            sp.wait_ge(s["x2"], PAIRS * ROUNDS * GROUP)
            store(out, (ROUNDS - 1) * GROUP)
            sp.wait_ge(s["stored"], 16 * (PAIRS * ROUNDS + 1))

        @block.gpsimd
        def _(pool):
            pool.memset(minus_half[:], -0.5)
            pool.memset(ones3[:], 1.0)
            pool.memset(vaug[:], 1.0)
            pool.memset(haug[:], 1.0).then_inc(s["setup_pool"], 1)
            pool.wait_ge(s["setup_pool"], 1)

            def layernorm(r, kind, i, b):
                hold(pool, s[kind + "_mv"], done(r, b))
                pool.tensor_scalar(var_eps[:, i, b:b + 1], mv[:, i, b, 1:2], EPS, None, ALU.add).then_inc(s[kind + "_var"], 1)
                pool.wait_ge(s[kind + "_var"], done(r, b))
                pool.tensor_tensor(rstd[:, i, b:b + 1], var_eps[:, i, b:b + 1], minus_half[:], ALU.pow).then_inc(s[kind + "_rstd"], 1)
                hold(pool, s[kind + "_rstd"], done(r, b))
                pool.tensor_scalar(shift[:, i, b:b + 1], mv[:, i, b, 0:1], rstd[:, i, b:b + 1], -1.0, ALU.mult, ALU.mult).then_inc(s[kind + "_shift"], 1)

            with pool.Fori(0, PAIRS) as p:
                v_in = pool.snap(p * 48 + 48)
                with pool.Fori(0, ROUNDS) as g:
                    r = Round(pool, p, g)
                    hold(pool, s["adj_in"], r.dma)
                    pool.tensor_scalar(neg_bias[:], adj8[:], -1.0, -NEG, ALU.add, ALU.mult)
                    pool.tensor_scalar(no_edge[:], adj8[:], -1.0, 1.0, ALU.mult, ALU.add)
                    pool.tensor_scalar(floor[:], adj8[:], LEAST, NO_EDGE, ALU.mult, ALU.add).then_inc(s["masks"], 1)
                    for b in range(GROUP):
                        layernorm(r, "m", 0, b)
                    hold(pool, s["v_in"], v_in)
                    for b in range(GROUP):
                        pool.wait_ge(s["m_h"], done(r, b))
                        pool.tensor_tensor(xin[:, b, :], xin[:, b, :], bf_bc, ALU.add).then_inc(s["xb"], 1)
                    for b in range(GROUP):
                        layernorm(r, "g", 1, b)
                    for b in range(GROUP):
                        pool.wait_ge(s["g_th"], done(r, b))
                        if b >= 1:
                            pool.wait_ge(s["g_sd"], done(r, b - 1))
                        for k in range(2):
                            last = pool.tensor_tensor(prod[:, k, :], th[:, b, :], vec[:, 3 + k, :], ALU.mult)
                        last.then_inc(s["g_prod"], 1)
                        hold(pool, s["g_sd"], done(r, b))
                        j = b % 2
                        if b >= 2:
                            hold(pool, s["g_sdT_ps"], done(r, b - 2))
                        pool.tensor_copy(sd3[:, j, 0, :], sd[:, j, :]).then_inc(s["g_sd_hi"], 1)
                        pool.wait_ge(s["g_sd_hi"], done(r, b))
                        pool.tensor_tensor(sd_rest[:, j, 0, :], sd[:, j, :], sd3[:, j, 0, :], ALU.subtract).then_inc(s["g_rest1"], 1)
                        hold(pool, s["g_rest1"], done(r, b))
                        pool.tensor_copy(sd3[:, j, 1, :], sd_rest[:, j, 0, :]).then_inc(s["g_sd_mid"], 1)
                        pool.wait_ge(s["g_sd_mid"], done(r, b))
                        pool.tensor_tensor(sd_rest[:, j, 1, :], sd_rest[:, j, 0, :], sd3[:, j, 1, :], ALU.subtract).then_inc(s["g_rest2"], 1)
                        hold(pool, s["g_rest2"], done(r, b))
                        pool.tensor_copy(sd3[:, j, 2, :], sd_rest[:, j, 1, :]).then_inc(s["g_sd3"], 1)
                    for b in range(GROUP):
                        pool.wait_ge(s["g_h"], done(r, b))
                        pool.tensor_tensor(x1[:, b, :], x1[:, b, :], hG[:, b, :], ALU.add).then_inc(s["xf"], 1)
                    for b in range(GROUP):
                        hold(pool, s["pv_norm"], done(r, b))
                        pool.tensor_scalar(ey[:, b % 2, :], y[:, b % 2, :], 0.0, None, ALU.min).then_inc(s["y_min"], 1)

        @block.scalar
        def _(act):
            def normed(r, kind, i, b, src, dst):
                act.wait_ge(s[kind + "_shift"], done(r, b))
                act.activation(dst[:, b, :], src[:, b, :], ACT.Relu, bias=shift[:, i, b:b + 1],
                               scale=rstd[:, i, b:b + 1]).then_inc(s[kind + "_h"], 1)

            def hi_half(r, kind, b):
                act.wait_ge(s[kind + "_hT"], done(r, b))
                act.activation(hT_hi[:, :, b, :], bank(4 + b % 2)[:, 0:D].rearrange("p (c n) -> p c n", c=KC),
                               ACT.Copy).then_inc(s[kind + "_hi"], 1)

            with act.Fori(0, PAIRS) as p:
                v_in = act.snap(p * 48 + 48)
                v1 = act.snap(p + 1)
                act.wait_ge(s["v_in"], v_in)
                act.activation(q_bias8[:], qk_bias[:, 0:KC], ACT.Copy, scale=MD ** -0.5).then_inc(s["setup_act"], 1)
                act.wait_ge(s["setup_act"], v1)
                with act.Fori(0, ROUNDS) as g:
                    r = Round(act, p, g)
                    for b in range(GROUP):
                        normed(r, "m", 0, b, xin, hM)
                    for b in range(GROUP):
                        hi_half(r, "m", b)
                    for c in [0, 3, 1, 4, 2, 5]:
                        act.wait_ge(qk_ps[c], r.one)
                        q = c < KC
                        act.activation(QKT[:, c, :], bank([0, 3, 1, 4, 2, 5].index(c) % 4), ACT.Identity,
                                       bias=q_bias8[:, c:c + 1] if q else qk_bias[:, c:c + 1],
                                       scale=MD ** -0.5 if q else 1.0).then_inc(qk[c], 1)
                    for k in range(GROUP + 2):
                        if k >= 2:
                            b = k - 2
                            act.wait_ge(s["cT_ps"], done(r, b))
                            act.activation(cT_hi[:, b % 2, :, :], bank(7)[:, 0:D].rearrange("p (c n) -> p c n", c=KC),
                                           ACT.Copy).then_inc(s["cT_hi"], 1)
                        if 1 <= k <= GROUP:
                            b = k - 1
                            act.wait_ge(s["pt_ps"], done(r, b))
                            act.activation(PT[:, b % 2, 0:MH * N].rearrange("p (e n) -> p e n", e=2),
                                           banks(4, 2)[:, :, 0:D], ACT.Copy).then_inc(s["pt"], 1)
                        if k < GROUP:
                            act.wait_ge(s["s_shifted"], done(r, k))
                            act.activation(L[:, k % LSLOTS, 0:MH * N], L[:, k % LSLOTS, 0:MH * N], ACT.Exp).then_inc(s["s_exp"], 1)
                        if k >= 2:
                            normed(r, "g", 1, k - 2, x1, hG)
                    for b in range(GROUP):
                        hi_half(r, "g", b)
                    for b in range(GROUP):
                        act.wait_ge(s["g_h_ps"], done(r, b))
                        act.activation(th[:, b, :], bank(b % 2)[:, 0:D], ACT.Tanh).then_inc(s["g_th"], 1)
                        act.wait_ge(s["g_gate_ps"], done(r, b))
                        act.activation(gate[:, b, :], bank(2 + b % 2)[:, 0:D], ACT.Tanh, scale=0.5).then_inc(s["g_gate"], 1)
                    for k in range(GROUP + 3):
                        if k < GROUP:
                            act.wait_ge(s["g_sdT_ps"], done(r, k))
                            act.activation(sdT[:, k % 2, :], sdT_ps, ACT.Copy).then_inc(s["g_sdT"], 1)
                            act.wait_ge(s["z_ps"], done(r, k))
                            act.activation(L[:, k % LSLOTS, :].rearrange("p (e n) -> p e n", e=3), banks(0, 3),
                                           ACT.Copy, scale=SLOPE).then_inc(s["z_slope"], 1)
                        if 1 <= k <= GROUP:
                            b = k - 1
                            act.wait_ge(s["z_shifted"], done(r, b))
                            act.activation(L[:, b % LSLOTS, :], L[:, b % LSLOTS, :], ACT.Exp).then_inc(s["z_exp"], 1)
                        if 2 <= k <= GROUP + 1:
                            b = k - 2
                            act.wait_ge(s["gpt_ps"], done(r, b))
                            act.activation(PT[:, b % 2, :].rearrange("p (e n) -> p e n", e=3), banks(3, 3),
                                           ACT.Copy).then_inc(s["gpt"], 1)
                        if k >= 3:
                            b = k - 3
                            act.wait_ge(s["y_min"], done(r, b))
                            act.activation(ey[:, b % 2, :], ey[:, b % 2, :], ACT.Exp).then_inc(s["y_exp"], 1)

        @block.vector
        def _(dve):
            dve.wait_ge(s["const_in"], 32)
            dve.tensor_copy(idb[:], idf[:])
            dve.tensor_scalar(far_id[:], idf[:], -FAR, None, ALU.mult)
            dve.tensor_copy(sel_s[:].rearrange("c a n -> c (a n)"), stage[0:PARTS * SD, 0:2, :].rearrange("c k n -> c (k n)")).then_inc(s["setup_dve"], 1)
            dve.wait_ge(s["const_in"], 48)
            dve.tensor_copy(sel_d[:].rearrange("c a n -> c (a n)"), stage[0:PARTS * SD, 0:2, :].rearrange("c k n -> c (k n)")).then_inc(s["setup_dve"], 1)
            dve.wait_ge(s["setup_dve"], 2)

            def statistics(r, kind, i, b, src):
                dve.bn_stats(stats[:, i, b, :], src[:, b, :]).then_inc(s[kind + "_stats"], 1)
                hold(dve, s[kind + "_stats"], done(r, b))
                dve.bn_aggr(mv[:, i, b, :], stats[:, i, b, :]).then_inc(s[kind + "_mv"], 1)

            def lo_half(r, kind, b):
                dve.wait_ge(s[kind + "_hi"], done(r, b))
                dve.tensor_tensor(hT_lo[:, :, b, :], bank(4 + b % 2)[:, 0:D].rearrange("p (c n) -> p c n", c=KC),
                                  hT_hi[:, :, b, :].bitcast(F32), ALU.subtract).then_inc(s[kind + "_lo"], 1)

            with dve.Fori(0, PAIRS) as p:
                v_in = dve.snap(p * 48 + 48)
                for i, (hi, lo) in enumerate(((qk_hi, qk_lo), (vf_hi, vf_lo), (hg_hi, hg_lo))):
                    w_in = dve.snap(p * 48 + 16 * (i + 1))
                    k1 = dve.snap(p * 3 + i + 1)
                    dve.wait_ge(s["w_in"], w_in)
                    dve.tensor_copy(hi[:], stage[:]).then_inc(s["w_ready_dve"], 1)
                    dve.wait_ge(s["w_ready_dve"], k1)
                    dve.tensor_tensor(lo[:], stage[:], hi[:].bitcast(F32), ALU.subtract).then_inc(s["stage_split"], 1)
                step = [dve.snap(p * 8 + k) for k in range(1, 9)]
                dve.wait_ge(s["v_in"], v_in)
                dve.tensor_copy(hb_part[:, 0, :], hb_row[:]).then_inc(s["hb_step"], 1)
                dve.wait_ge(s["hb_step"], step[0])
                dve.tensor_tensor(hb_rest[:], hb_row[:], hb_part[:, 0, :], ALU.subtract).then_inc(s["hb_step"], 1)
                dve.wait_ge(s["hb_step"], step[1])
                dve.tensor_copy(hb_part[:, 1, :], hb_rest[:]).then_inc(s["hb_step"], 1)
                dve.wait_ge(s["hb_step"], step[2])
                dve.tensor_tensor(hb_rest[:], hb_rest[:], hb_part[:, 1, :], ALU.subtract).then_inc(s["hb_step"], 1)
                dve.wait_ge(s["hb_step"], step[3])
                dve.tensor_copy(hb_part[:, 2, :], hb_rest[:])
                dve.tensor_scalar(hb_acc[:], hb_part[:, 0, :], idf[0:PARTS, 0:1], None, ALU.mult).then_inc(s["hb_step"], 1)
                dve.wait_ge(s["hb_step"], step[4])
                dve.scalar_tensor_tensor(hb_acc[:], hb_part[:, 1, :], idf[0:PARTS, 1:2], hb_acc[:], ALU.mult, ALU.add).then_inc(s["hb_step"], 1)
                dve.wait_ge(s["hb_step"], step[5])
                dve.scalar_tensor_tensor(hb3[:], hb_part[:, 2, :], idf[0:PARTS, 2:3], hb_acc[:], ALU.mult, ALU.add).then_inc(s["hb_step"], 2)

                with dve.Fori(0, ROUNDS) as g:
                    r = Round(dve, p, g)
                    dve.wait_ge(s["x_in"], r.dma)
                    for b in range(GROUP):
                        statistics(r, "m", 0, b, xin)
                    for b in range(GROUP):
                        lo_half(r, "m", b)
                    for b in range(GROUP):
                        dve.wait_ge(s["m_v"], done(r, b))
                        dve.tensor_tensor(vaug[:, b, :, 0:MD], bank(6 + b % 2)[:, 0:D].rearrange("p (h d) -> p h d", h=MH),
                                          bv_bc.rearrange("p (h d) -> p h d", h=MH), ALU.add).then_inc(s["m_vaug"], 1)
                    for k in range(GROUP + 2):
                        if k < GROUP:
                            Sb = L[:, k % LSLOTS, 0:MH * N].rearrange("p (h n) -> p h n", h=MH)
                            dve.wait_ge(s["s_ps"], done(r, k))
                            if k == 0:
                                dve.wait_ge(s["masks"], r.one)
                            dve.tensor_tensor(L[:, k % LSLOTS, 0:MH * N].rearrange("p (e h n) -> p e h n", e=2, h=KC),
                                              banks(2 * (k % 2), 2)[:, :, 0:D].rearrange("p e (h n) -> p e h n", h=KC),
                                              neg_bias[:, k, :].unsqueeze(1).unsqueeze(1).broadcast_to([128, 2, KC, N]),
                                              ALU.add).then_inc(s["s_biased"], 1)
                            dve.wait_ge(s["s_biased"], done(r, k))
                            dve.tensor_reduce(mx[:, 0, 0:MH], Sb, AX.X, ALU.max).then_inc(s["s_max"], 1)
                            dve.wait_ge(s["s_max"], done(r, k))
                            dve.tensor_tensor(Sb, Sb, mx[:, 0, 0:MH].unsqueeze(2).broadcast_to([128, MH, N]),
                                              ALU.subtract).then_inc(s["s_shifted"], 1)
                        if 1 <= k <= GROUP:
                            b = k - 1
                            c_ps = bank(6)[:, 0:MH * (MD + 1)].rearrange("p (h d) -> p h d", h=MH)
                            dve.wait_ge(s["c_ps"], done(r, b))
                            dve.reciprocal(rden[:, 0, 0:MH].unsqueeze(2), c_ps[:, :, MD:MD + 1]).then_inc(s["c_rden"], 1)
                            dve.wait_ge(s["c_rden"], done(r, b))
                            dve.tensor_tensor(ctxn[:, b % 2, :].rearrange("p (h d) -> p h d", h=MH), c_ps[:, :, 0:MD],
                                              rden[:, 0, 0:MH].unsqueeze(2).broadcast_to([128, MH, MD]),
                                              ALU.mult).then_inc(s["c_norm"], 1)
                        if k >= 2:
                            b = k - 2
                            dve.wait_ge(s["cT_hi"], done(r, b))
                            dve.tensor_tensor(cT_lo[:], bank(7)[:, 0:D].rearrange("p (c n) -> p c n", c=KC),
                                              cT_hi[:, b % 2, :, :].bitcast(F32), ALU.subtract).then_inc(s["cT_lo"], 1)
                            dve.wait_ge(s["o_ps"], done(r, b))
                            if b == 0:
                                dve.wait_ge(s["stored"], r.dma)
                            dve.wait_ge(s["xb"], done(r, b))
                            dve.tensor_tensor(x1[:, b, :], bank(7)[:, 0:D], xin[:, b, :], ALU.add).then_inc(s["x1"], 1)
                            dve.wait_ge(s["x1"], done(r, b))
                            statistics(r, "g", 1, b, x1)
                    for b in range(GROUP):
                        lo_half(r, "g", b)
                    for b in range(GROUP):
                        dve.wait_ge(s["g_th"], done(r, b))
                        dve.tensor_tensor(haug[:, b, :, 0:GD], bank(b % 2)[:, 0:D].rearrange("p (a e) -> p a e", a=GH),
                                          bg_bc.rearrange("p (a e) -> p a e", a=GH), ALU.add).then_inc(s["g_haug"], 1)
                        dve.wait_ge(s["g_prod"], done(r, b))
                        if b >= 2:
                            dve.wait_ge(s["g_rest1"], done(r, b - 2))
                        dve.tensor_reduce(sd[:, b % 2, :], prod[:].rearrange("p k (a e) -> p (k a) e", a=GH), AX.X,
                                          ALU.add).then_inc(s["g_sd"], 1)
                    for k in range(GROUP + 3):
                        if k < GROUP:
                            Lk = L[:, k % LSLOTS, :].rearrange("p (a n) -> p a n", a=GH)
                            dve.wait_ge(s["z_slope"], done(r, k))
                            dve.tensor_tensor(L[:, k % LSLOTS, :].rearrange("p (e n) -> p e n", e=3), banks(0, 3),
                                              L[:, k % LSLOTS, :].rearrange("p (e n) -> p e n", e=3), ALU.max).then_inc(s["z_leaky"], 1)
                            dve.wait_ge(s["z_leaky"], done(r, k))
                            dve.tensor_tensor(Lk, Lk, floor[:, k, :].unsqueeze(1).broadcast_to([128, GH, N]),
                                              ALU.max).then_inc(s["z_masked"], 1)
                            dve.wait_ge(s["z_masked"], done(r, k))
                            dve.tensor_reduce(mx[:, 1, :], Lk, AX.X, ALU.max).then_inc(s["z_max"], 1)
                            dve.wait_ge(s["z_max"], done(r, k))
                            dve.tensor_tensor(Lk, Lk, mx[:, 1, :].unsqueeze(2).broadcast_to([128, GH, N]),
                                              ALU.subtract).then_inc(s["z_shifted"], 1)
                        if 2 <= k <= GROUP + 1:
                            b = k - 2
                            pv = bank(6)[:, 0:GH * (GD + 1)].rearrange("p (a e) -> p a e", a=GH)
                            dve.wait_ge(s["pv_ps"], done(r, b))
                            dve.reciprocal(rden[:, 1, :].unsqueeze(2), pv[:, :, GD:GD + 1]).then_inc(s["pv_rden"], 1)
                            dve.wait_ge(s["pv_rden"], done(r, b))
                            dve.tensor_tensor(y[:, b % 2, :].rearrange("p (a e) -> p a e", a=GH), pv[:, :, 0:GD],
                                              rden[:, 1, :].unsqueeze(2).broadcast_to([128, GH, GD]),
                                              ALU.mult).then_inc(s["pv_norm"], 1)
                        if k >= 3:
                            b = k - 3
                            yb = y[:, b % 2, :]
                            dve.wait_ge(s["y_exp"], done(r, b))
                            dve.scalar_tensor_tensor(yb, yb, 0.0, ey[:, b % 2, :], ALU.max, ALU.add).then_inc(s["elu"], 1)
                            dve.wait_ge(s["elu"], done(r, b))
                            dve.scalar_tensor_tensor(yb, yb, -1.0, hG[:, b, :], ALU.add, ALU.subtract).then_inc(s["elu_f"], 1)
                            dve.wait_ge(s["elu_f"], done(r, b))
                            dve.wait_ge(s["g_gate"], done(r, b))
                            dve.scalar_tensor_tensor(yb, gate[:, b, :], 1.0, yb, ALU.add, ALU.mult).then_inc(s["mixed"], 1)
                            dve.wait_ge(s["mixed"], done(r, b))
                            dve.wait_ge(s["xf"], done(r, b))
                            dve.scalar_tensor_tensor(x1[:, b, :], yb, 0.5, x1[:, b, :], ALU.mult, ALU.add).then_inc(s["x2"], 1)

        @block.tensor
        def _(pe):
            pe.wait_ge(s["setup_dve"], 2)
            pe.wait_ge(s["setup_pool"], 1)

            def features(src, dst):
                for c in range(KC):
                    last = pe.transpose(dst[:, c * 128:(c + 1) * 128], src[:, c * 128:(c + 1) * 128], idf[:])
                return last

            def tokens_times(dst, hi, lo, w_hi, w_lo, at, begun=False):
                n = 0
                for a, w in ((hi, w_hi), (hi, w_lo), (lo, w_hi)):
                    for c in range(KC):
                        last = pe.matmul(dst, a(c), w[:, c, at:at + D], start=(n == 0 and not begun), stop=(n == 3 * KC - 1))
                        n += 1
                return last

            with pe.Fori(0, PAIRS) as p:
                split = pe.snap(p * 3 + 3)
                hb_done = pe.snap(p * 8 + 8)
                hold(pe, s["stage_split"], split)
                hold(pe, s["hb_step"], hb_done)
                with pe.Fori(0, ROUNDS) as g:
                    r = Round(pe, p, g)
                    for b in range(GROUP):
                        pe.wait_ge(s["m_h"], done(r, b))
                        if b >= 2:
                            pe.wait_ge(s["m_lo"], done(r, b - 2))
                        features(hM[:, b, :], bank(4 + b % 2)).then_inc(s["m_hT"], 1)
                    for b in range(GROUP):
                        pe.wait_ge(s["m_lo"], done(r, b))
                        if b >= 2:
                            pe.wait_ge(s["m_vaug"], done(r, b - 2))
                        tokens_times(bank(6 + b % 2)[:, 0:D], lambda c: hT_hi[:, c, b, :], lambda c: hT_lo[:, c, b, :],
                                     vf_hi, vf_lo, 0).then_inc(s["m_v"], 1)
                    order = [0, 3, 1, 4, 2, 5]
                    for k, c in enumerate(order):
                        if k >= 4:
                            pe.wait_ge(qk[order[k - 4]], r.one)
                        n = 0
                        for w, a in ((qk_hi, hT_hi), (qk_lo, hT_hi), (qk_hi, hT_lo)):
                            for i in range(KC):
                                last = pe.matmul(bank(k % 4), w[:, i, c * 128:(c + 1) * 128],
                                                 a[:, i, :, :].rearrange("p b n -> p (b n)"), start=(n == 0), stop=(n == 3 * KC - 1))
                                n += 1
                        last.then_inc(qk_ps[c], 1)
                    for k in range(GROUP + 2):
                        if k < GROUP:
                            if k == 0:
                                for c in order:
                                    pe.wait_ge(qk[c], r.one)
                            if k >= 2:
                                pe.wait_ge(s["s_biased"], done(r, k - 2))
                            for i in range(MH):
                                h = head_of(i)
                                rows = slice(64 * (h % 2), 64 * (h % 2) + 64)
                                last = pe.matmul(bank(2 * (k % 2) + i // KC)[:, (i % KC) * N:(i % KC + 1) * N],
                                                 QKT[rows, h // 2, k * N:(k + 1) * N], QKT[rows, KC + h // 2, k * N:(k + 1) * N],
                                                 start=True, stop=True)
                            last.then_inc(s["s_ps"], 1)
                        if k >= 2:
                            b = k - 2
                            pe.wait_ge(s["c_norm"], done(r, b))
                            if b >= 1:
                                pe.wait_ge(s["x1"], done(r, b - 1))
                            else:
                                pe.wait_ge(s["m_vaug"], done(r, 3))
                            features(ctxn[:, b % 2, :], bank(7)).then_inc(s["cT_ps"], 1)
                        if 1 <= k <= GROUP:
                            b = k - 1
                            pe.wait_ge(s["s_exp"], done(r, b))
                            if b >= 1:
                                pe.wait_ge(s["pt"], done(r, b - 1))
                            for i in range(MH):
                                last = pe.transpose(bank(4 + i // KC)[:, (i % KC) * N:(i % KC + 1) * N],
                                                    L[:, b % LSLOTS, i * N:(i + 1) * N], idf[:])
                            last.then_inc(s["pt_ps"], 1)
                            pe.wait_ge(s["pt"], done(r, b))
                            pe.wait_ge(s["m_vaug"], done(r, 3))
                            if b >= 1:
                                pe.wait_ge(s["c_norm"], done(r, b - 1))
                            for i in range(MH):
                                h = head_of(i)
                                last = pe.matmul(bank(6)[:, h * (MD + 1):(h + 1) * (MD + 1)], PT[:, b % 2, i * N:(i + 1) * N],
                                                 vaug[:, b, h, :], start=True, stop=True)
                            last.then_inc(s["c_ps"], 1)
                        if k >= 2:
                            b = k - 2
                            pe.wait_ge(s["cT_lo"], done(r, b))
                            tokens_times(bank(7)[:, 0:D], lambda c: cT_hi[:, b % 2, c, :], lambda c: cT_lo[:, c, :],
                                         vf_hi, vf_lo, D).then_inc(s["o_ps"], 1)
                    for b in range(GROUP):
                        pe.wait_ge(s["g_h"], done(r, b))
                        if b >= 2:
                            pe.wait_ge(s["g_lo"], done(r, b - 2))
                        features(hG[:, b, :], bank(4 + b % 2)).then_inc(s["g_hT"], 1)
                    for b in range(GROUP):
                        pe.wait_ge(s["g_lo"], done(r, b))
                        if b >= 2:
                            pe.wait_ge(s["g_haug"], done(r, b - 2))
                        else:
                            pe.wait_ge(s["s_biased"], done(r, 3))
                        tokens_times(bank(b % 2)[:, 0:D], lambda c: hT_hi[:, c, b, :], lambda c: hT_lo[:, c, b, :],
                                     hg_hi, hg_lo, 0).then_inc(s["g_h_ps"], 1)
                        if b >= 2:
                            pe.wait_ge(s["g_gate"], done(r, b - 2))
                        pe.matmul(bank(2 + b % 2)[:, 0:D], ones3[:], hb3[:], start=True, stop=False)
                        tokens_times(bank(2 + b % 2)[:, 0:D], lambda c: hT_hi[:, c, b, :], lambda c: hT_lo[:, c, b, :],
                                     hg_hi, hg_lo, D, begun=True).then_inc(s["g_gate_ps"], 1)
                    for k in range(GROUP + 2):
                        if k < GROUP:
                            pe.wait_ge(s["g_sd3"], done(r, k))
                            if k >= 1:
                                pe.wait_ge(s["g_sdT"], done(r, k - 1))
                            pe.transpose(sdT_ps, sd3[:, k % 2, :, :].rearrange("p a n -> p (a n)"), idb[:]).then_inc(s["g_sdT_ps"], 1)
                            if k >= 1:
                                pe.wait_ge(s["z_leaky"], done(r, k - 1))
                            else:
                                pe.wait_ge(s["g_haug"], done(r, 3))
                                pe.wait_ge(s["g_gate"], done(r, 3))
                            pe.wait_ge(s["g_sdT"], done(r, k))
                            for q in range(3):
                                four = bank(q).rearrange("p (a n) -> p a n", a=4)
                                pe.matmul(four, sdT[:, k % 2, :], sel_s[:, 4 * q:4 * q + 4, :], start=True, stop=False)
                                for a in range(4):
                                    pe.matmul(four[:, a, :], sel_d[:, 4 * q + a, :], sdT[:, k % 2, :], start=False, stop=False)
                                last = pe.matmul(four, far_id[:], no_edge[:, k, :].unsqueeze(1).broadcast_to([128, 4, N]),
                                                 start=False, stop=True)
                            last.then_inc(s["z_ps"], 1)
                        if k >= 2:
                            b = k - 2
                            pe.wait_ge(s["z_exp"], done(r, b))
                            if b >= 1:
                                pe.wait_ge(s["gpt"], done(r, b - 1))
                            for a in range(GH):
                                last = pe.transpose(bank(3 + a // 4)[:, (a % 4) * N:(a % 4 + 1) * N],
                                                    L[:, b % LSLOTS, a * N:(a + 1) * N], idf[:])
                            last.then_inc(s["gpt_ps"], 1)
                            pe.wait_ge(s["gpt"], done(r, b))
                            if b >= 1:
                                pe.wait_ge(s["pv_norm"], done(r, b - 1))
                            for a in range(GH):
                                last = pe.matmul(bank(6)[:, a * (GD + 1):(a + 1) * (GD + 1)], PT[:, b % 2, a * N:(a + 1) * N],
                                                 haug[:, b, a, :], start=True, stop=True)
                            last.then_inc(s["pv_ps"], 1)


def kernel(**inputs):
    import numpy as np
    import concourse.bacc as bacc
    from concourse.bass_utils import run_bass_kernel_spmd as run

    def of(layer, name):
        return np.asarray(inputs[f"L{layer}_gnn_{name}"])

    w_qk = np.stack([np.concatenate([of(m, "Wq"), of(m, "Wk")], 1) for m in (0, 2)])
    w_vf = np.stack([np.concatenate([of(m, "Wv"), of(m, "Wf")], 1) for m in (0, 2)])
    w_hg = np.stack([np.concatenate([of(g, "W").transpose(1, 0, 2).reshape(D, D), of(g, "H_w").T], 1) for g in (1, 3)])
    b_qk = np.stack([np.concatenate([of(m, "bq"), of(m, "bk")]).reshape(2 * KC, 128).T for m in (0, 2)])
    vecs = np.stack([np.stack([of(g - 1, "bv"), of(g - 1, "bf"), np.tile(of(g, "b"), GH),
                               of(g, "w_src").reshape(D), of(g, "w_dst").reshape(D)]) for g in (1, 3)])
    h_b = np.stack([of(g, "H_b") for g in (1, 3)])
    row = np.arange(PARTS * SD)[:, None, None]
    head = np.arange(GH)[None, :, None]
    sel_src = np.broadcast_to(row % SD == head, (PARTS * SD, GH, 128)).astype(np.float32).reshape(PARTS * SD, GH * 128)
    sel_dst = np.broadcast_to(row % SD == GH + head, (PARTS * SD, GH, 128)).astype(np.float32).reshape(PARTS * SD, GH * 128)
    arrays = {
        "x": np.asarray(inputs["x"]), "adj": np.asarray(inputs["adj"]), "w_qk": w_qk, "w_vf": w_vf, "w_hg": w_hg,
        "b_qk": b_qk, "vecs": vecs, "h_b": h_b, "ident": np.eye(128, dtype=np.float32), "sel_src": sel_src, "sel_dst": sel_dst,
    }
    nc = bacc.Bacc("TRN2", target_bir_lowering=False, num_devices=1)
    args = []
    for name, a in arrays.items():
        arrays[name] = a = np.ascontiguousarray(a)
        args.append(nc.dram_tensor(name, a.shape, mybir.dt.from_np(a.dtype), kind="ExternalInput").ap())
    args.append(nc.dram_tensor("out", inputs["x"].shape, F32, kind="ExternalOutput").ap())
    graph_stack(nc, *args)
    r = run(nc, [arrays], core_ids=[0])
    return r.results[0]["out"]
```

```python
from contextlib import ExitStack

import concourse.bass as bass
from concourse import mybir

F32 = mybir.dt.float32
F32R = mybir.dt.float32r
BF16 = mybir.dt.bfloat16
U8 = mybir.dt.uint8
ALU = mybir.AluOpType
ACT = mybir.ActivationFunctionType
AX = mybir.AxisListType

SLOTS = 8
PAIRS = 2
N = 128
D = 384
KC = D // 128
MH, MD = 6, 64
GH, GD = 12, 32
QUADS = GH // 4
NEG = -9000000000000000.0
NO_EDGE = -999.0
SLOPE = 0.2
FAR = float(2.0**126)
LEAST = -3.0e38
EPS = 1e-5
PARTS = 3
SD = 2 * GH
HALF_SLOTS = SLOTS // 2
QK_ORDER = [0, 3, 1, 4, 2, 5]

FIRST_STEP, STEPS_BEHIND = -5, 6


def graph_stack(nc, x, adj, w_qk, w_vf, w_hg, b_cols, vecs, h_b, ident, sel_src, sel_dst, out):
    B = x.shape[0]

    with ExitStack() as ctx:
        def sb(name, shape, dt=F32):
            return ctx.enter_context(nc.sbuf_tensor(name, shape, dt))

        def sem(name):
            return ctx.enter_context(nc.semaphore(name))

        x_mid = nc.dram_tensor("x_mid", x.shape, F32, kind="Internal").ap()

        qk_hi, qk_lo = sb("qk_hi", [128, KC, 2 * D], F32R), sb("qk_lo", [128, KC, 2 * D], F32R)
        vf_hi, vf_lo = sb("vf_hi", [128, KC, 2 * D], F32R), sb("vf_lo", [128, KC, 2 * D], F32R)
        hg_hi, hg_lo = sb("hg_hi", [128, KC, 2 * D], F32R), sb("hg_lo", [128, KC, 2 * D], F32R)
        vec = sb("vec", [128, 4, D])
        out_bias, bg_bc = vec[:, 0, :], vec[:, 1, :]
        cols = sb("cols", [128, 3 * KC])
        q_bias8 = sb("q_bias8", [128, KC])
        hb_row = sb("hb_row", [PARTS, D])
        hb3 = sb("hb3", [PARTS, D], BF16)

        idf = sb("idf", [128, 128])
        idb = sb("idb", [128, 128], BF16)
        far_id = sb("far_id", [128, 128], BF16)
        ones3 = sb("ones3", [PARTS, 128], BF16)
        sel_s = sb("sel_s", [PARTS * SD, GH, 128], BF16)
        sel_d = sb("sel_d", [PARTS * SD, GH, 128], BF16)
        minus_half = sb("minus_half", [128, 1])

        adj8 = sb("adj8", [128, SLOTS, N], U8)
        neg_bias = sb("neg_bias", [128, 2, N])
        floor = sb("floor", [128, 2, N])
        no_edge = sb("no_edge", [128, 2, N], BF16)
        xin = sb("xin", [128, SLOTS, D])
        x1 = sb("x1", [128, SLOTS, D])
        hM = sb("hM", [128, D])
        hG = sb("hG", [128, SLOTS, D])
        stats = sb("stats", [128, 2, SLOTS, 6])
        mv = sb("mv", [128, 2, SLOTS, 2])
        var_eps = sb("var_eps", [128, 2, SLOTS])
        rstd = sb("rstd", [128, 2, SLOTS])
        shift = sb("shift", [128, 2, SLOTS])
        hT_hi = sb("hT_hi", [128, KC, 4, N], F32R)
        hT_lo = sb("hT_lo", [128, KC, 4, N], F32R)
        gT_hi = sb("gT_hi", [128, KC, N], F32R)
        gT_lo = sb("gT_lo", [128, KC, N], F32R)
        QKT = sb("QKT", [128, 2 * KC, 4 * N])
        th = sb("th", [128, 2, D])
        gate = sb("gate", [128, 4, D])
        vaug = sb("vaug", [128, 4, MH, MD + 1])
        haug = sb("haug", [128, 4, GH, GD + 1])
        LA = sb("LA", [128, 2, MH * N])
        LG = sb("LG", [128, 2, GH * N])
        PTA = sb("PTA", [128, MH * N])
        PTG = sb("PTG", [128, QUADS, 4 * N])
        mx = sb("mx", [128, 2, GH])
        rden = sb("rden", [128, 2, GH])
        ctxn = sb("ctxn", [128, 2, D])
        cT_hi = sb("cT_hi", [128, KC, N], F32R)
        cT_lo = sb("cT_lo", [128, KC, N], F32R)
        prod = sb("prod", [128, 2, D])
        sd = sb("sd", [128, 4, SD])
        sd_rest = sb("sd_rest", [128, 4, 2, SD])
        sd3 = sb("sd3", [128, 4, PARTS, SD], BF16)
        sdT = sb("sdT", [PARTS * SD, 2, N], BF16)
        y = sb("y", [128, D])
        ey = sb("ey", [128, D])
        stages = [LG[:, 0, 0:KC * D].rearrange("p (c n) -> p c n", c=KC),
                  LA[:].rearrange("p a n -> p (a n)")[:, 0:KC * D].rearrange("p (c n) -> p c n", c=KC)]
        bv_cols = LG[:, 1, 0:D].rearrange("p (c n) -> p c n", c=KC)
        hb_rest, hb_acc = y[0:PARTS, :], ey[0:PARTS, :]
        hb_part = th[0:PARTS, :, :].rearrange("p a n -> p (a n)").bitcast(BF16).rearrange("p (k n) -> p k n", k=4)

        psum = ctx.enter_context(nc.psum_tensor("psum", [128, 8, 512], F32))
        sdT_ps = psum[0:PARTS * SD, 5, 512 - N // 2:512].bitcast(BF16)

        def bank(i):
            return psum[:, i, :]

        def banks(i, k):
            return psum[:, i:i + k, :]

        def chunks(ap):
            return ap[:, 0:D].rearrange("p (c n) -> p c n", c=KC)

        s = {n: sem(n) for n in (
            "v_in", "const_in", "stage_split", "setup_dve", "setup_act",
            "setup_pool", "hb_step", "w_hi", "bv_cols", "out_bias_ps", "out_bias", "bias_mask", "masks", "xb",
            "m_stats", "m_mv", "m_var", "m_rstd", "m_shift", "m_h", "m_hT", "m_hi", "m_lo", "m_v", "m_vaug",
            "qk_ps0", "qk_ps1", "qk_ps2", "qk0", "qk1", "qk2",
            "s_ps", "s_biased", "s_max", "s_shifted", "s_exp", "pt_ps", "pt", "c_ps", "c_rden", "c_norm",
            "cT_ps", "cT_hi", "cT_lo", "o_ps", "x1",
            "g_stats", "g_mv", "g_var", "g_rstd", "g_shift", "g_h", "g_hT", "g_hi", "g_lo", "g_h_ps", "g_gate_ps",
            "g_th", "g_gate", "g_haug", "g_prod", "g_sd", "g_sd_hi", "g_rest1", "g_sd_mid", "g_rest2", "g_sd3",
            "g_sdT_ps", "g_sdT", "z_ps", "z_slope", "z_leaky", "z_masked", "z_max", "z_shifted", "z_exp",
            "gpt_ps0", "gpt_ps1", "gpt_ps2", "gpt0", "gpt1", "gpt2",
            "pv_ps", "pv_rden", "pv_norm", "y_min", "y_exp", "xf", "elu", "elu_f", "mixed", "x2")}
        x_in = [sem(f"x_in{i}") for i in range(SLOTS)]
        stored = [sem(f"stored{i}") for i in range(SLOTS)]
        adj_in = [sem(f"adj_in{i}") for i in range(2)]
        w_in = [sem(f"w_in{i}") for i in range(2)]

        class Steps:

            def __init__(self, eng, base, visit, lowest, highest, dma=False):
                lo = -STEPS_BEHIND if lowest is None else 1
                hi = SLOTS + 5 if highest is None else highest + 1
                self.counts = {c: eng.snap(base + c) for c in range(lo, hi + 1)}
                self.lowest, self.highest = lowest, highest
                if dma:
                    self.dmas = {v: eng.snap(visit * 16 + 16 * (v + 1))
                                 for v in range(-1 if lowest is None else 0, 2 if highest is None else 1)}

            def has(self, g):
                return (self.lowest is None or g >= self.lowest) and (self.highest is None or g <= self.highest)

            def done(self, g):
                return self.counts[g + 1]

            def dma(self, g):
                return self.dmas[g // SLOTS]

        def hold(eng, semaphore, value):
            eng.wait_ge(semaphore, value)
            eng.nop(nofuse=True)

        def wait_latest(eng, r, *users):
            for name, g in users:
                if r.has(g):
                    eng.wait_ge(s[name], r.done(g))
                    return

        def head_of(i):
            return 2 * (i % KC) + i // KC

        def run_steps(eng, p, step, start=None, dma=False):
            r = Steps(eng, p * B, p * (B // SLOTS), 0, None, dma)
            for k in range(FIRST_STEP, SLOTS):
                if start:
                    start(r, k)
                step(r, k)
            with eng.Fori(1, B // SLOTS - 1) as g:
                r = Steps(eng, p * B + g * SLOTS, p * (B // SLOTS) + g, None, None, dma)
                for k in range(SLOTS):
                    step(r, k)
            r = Steps(eng, p * B + (B - SLOTS), p * (B // SLOTS) + (B // SLOTS - 1), None, SLOTS - 1, dma)
            for k in range(SLOTS + STEPS_BEHIND):
                step(r, k)

        block = ctx.enter_context(nc.Block())

        @block.sync
        def _(sp):
            sp.dma_start(idf[:], ident).then_inc(s["const_in"], 16)
            for i, src in enumerate((sel_src, sel_dst)):
                sp.dma_start(LG[0:PARTS * SD, i, :], src).then_inc(s["const_in"], 16)
            for i in range(SLOTS):
                sp.sem_inc(stored[i], 16)

            def load_x(src, g, slot):
                sp.dma_start(xin[:, slot:slot + 1, :], src[bass.ds(g, 1), :, :].rearrange("b p n -> p b n")).then_inc(x_in[slot], 16)

            def load_adj(g, half):
                sp.dma_start(adj8[:, half * HALF_SLOTS:(half + 1) * HALF_SLOTS, :],
                             adj[bass.ds(g, HALF_SLOTS), :, :].rearrange("b p n -> p b n")).then_inc(adj_in[half], 16)

            for pair, (src, dst) in enumerate(((x, x_mid), (x_mid, out))):
                if pair == 0:
                    for i in range(SLOTS):
                        load_x(x, i, i)
                    for half in range(2):
                        load_adj(half * HALF_SLOTS, half)
                n = 0
                for w in (w_qk, w_vf, w_hg):
                    for half in range(2):
                        if n >= 2:
                            sp.wait_ge(s["stage_split"], 6 * pair + n - 1)
                        elif pair:
                            sp.wait_ge(s["x2"], B)
                        else:
                            sp.wait_ge(s["setup_dve"], 2)
                        sp.dma_start(stages[n % 2], w[pair][:, half * D:(half + 1) * D].rearrange("(c p) n -> p c n", p=128)
                                     ).then_inc(w_in[n % 2], 16)
                        n += 1
                        if n == 2:
                            sp.dma_start(vec[:], vecs[pair].partition_broadcast(128)).then_inc(s["v_in"], 16)
                            sp.dma_start(cols[:], b_cols[pair]).then_inc(s["v_in"], 16)
                            sp.dma_start(hb_row[:], h_b[pair].partition_broadcast(PARTS)).then_inc(s["v_in"], 16)

                def move(k, base, count, filling, draining):
                    g = k + 6
                    if k >= 2 or not filling:
                        if not draining or g < SLOTS:
                            hold(sp, s["xb"], count(k - 1))
                            load_x(src, base + g, g % SLOTS)
                        elif pair == 0 and g < 2 * SLOTS:
                            hold(sp, s["xb"], count(k - 1))
                            sp.wait_ge(stored[g % SLOTS], 16 + 16)
                            load_x(x_mid, g % SLOTS, g % SLOTS)
                    g = k + 2
                    if g % HALF_SLOTS == 0 and (k >= 6 or not filling):
                        half = g // HALF_SLOTS % 2
                        if not draining or g < SLOTS:
                            hold(sp, s["masks"], count(k - 2))
                            load_adj(base + g, half)
                        elif pair == 0 and g < 2 * SLOTS:
                            hold(sp, s["masks"], count(k - 2))
                            load_adj(g % SLOTS, half)
                    if k >= 6 or not filling:
                        hold(sp, s["x2"], count(k - 5))
                        sp.dma_start(dst[bass.ds(base + k - 6, 1), :, :].rearrange("b p n -> p b n"),
                                     x1[:, (k - 6) % SLOTS:(k - 6) % SLOTS + 1, :]).then_inc(stored[(k - 6) % SLOTS], 16)

                for k in range(SLOTS):
                    move(k, 0, lambda c: pair * B + c, True, False)
                with sp.Fori(1, B // SLOTS - 1) as g:
                    base = sp.snap(g * SLOTS)
                    counts = {c: sp.snap(g * SLOTS + (pair * B + c)) for c in range(-5, SLOTS)}
                    for k in range(SLOTS):
                        move(k, base, counts.get, False, False)
                for k in range(SLOTS + STEPS_BEHIND):
                    move(k, B - SLOTS, lambda c: pair * B + B - SLOTS + c, False, True)
            for i in range(SLOTS):
                sp.wait_ge(stored[i], 16 * (PAIRS * B // SLOTS + 1))

        @block.gpsimd
        def _(pool):
            pool.memset(minus_half[:], -0.5)
            pool.memset(ones3[:], 1.0)
            pool.memset(vaug[:], 1.0)
            pool.memset(haug[:], 1.0).then_inc(s["setup_pool"], 1)
            pool.wait_ge(s["setup_pool"], 1)

            def layernorm(r, kind, i, g):
                b = g % SLOTS
                hold(pool, s[kind + "_mv"], r.done(g))
                pool.tensor_scalar(var_eps[:, i, b:b + 1], mv[:, i, b, 1:2], EPS, None, ALU.add).then_inc(s[kind + "_var"], 1)
                pool.wait_ge(s[kind + "_var"], r.done(g))
                pool.tensor_tensor(rstd[:, i, b:b + 1], var_eps[:, i, b:b + 1], minus_half[:], ALU.pow).then_inc(s[kind + "_rstd"], 1)
                hold(pool, s[kind + "_rstd"], r.done(g))
                pool.tensor_scalar(shift[:, i, b:b + 1], mv[:, i, b, 0:1], rstd[:, i, b:b + 1], -1.0, ALU.mult, ALU.mult
                                   ).then_inc(s[kind + "_shift"], 1)

            def score_parts(r, g):
                b = g % 4
                hold(pool, s["g_sd"], r.done(g))
                pool.tensor_copy(sd3[:, b, 0, :], sd[:, b, :]).then_inc(s["g_sd_hi"], 1)
                pool.wait_ge(s["g_sd_hi"], r.done(g))
                pool.tensor_tensor(sd_rest[:, b, 0, :], sd[:, b, :], sd3[:, b, 0, :], ALU.subtract).then_inc(s["g_rest1"], 1)
                hold(pool, s["g_rest1"], r.done(g))
                pool.tensor_copy(sd3[:, b, 1, :], sd_rest[:, b, 0, :]).then_inc(s["g_sd_mid"], 1)
                pool.wait_ge(s["g_sd_mid"], r.done(g))
                pool.tensor_tensor(sd_rest[:, b, 1, :], sd_rest[:, b, 0, :], sd3[:, b, 1, :], ALU.subtract).then_inc(s["g_rest2"], 1)
                hold(pool, s["g_rest2"], r.done(g))
                pool.tensor_copy(sd3[:, b, 2, :], sd_rest[:, b, 1, :]).then_inc(s["g_sd3"], 1)

            def step(r, k):
                if r.has(k - 6):
                    hold(pool, s["pv_norm"], r.done(k - 6))
                    pool.tensor_scalar(ey[:], y[:], 0.0, None, ALU.min).then_inc(s["y_min"], 1)
                if r.has(k - 2):
                    b = (k - 2) % SLOTS
                    pool.wait_ge(x_in[b], r.dma(k - 2))
                    pool.wait_ge(stored[b], r.dma(k - 2))
                    pool.tensor_tensor(x1[:, b, :], xin[:, b, :], out_bias, ALU.add).then_inc(s["xb"], 1)
                if r.has(k - 3):
                    b = (k - 3) % SLOTS
                    pool.wait_ge(s["g_h"], r.done(k - 3))
                    pool.tensor_tensor(x1[:, b, :], x1[:, b, :], hG[:, b, :], ALU.add).then_inc(s["xf"], 1)
                    pool.wait_ge(s["g_th"], r.done(k - 3))
                    if r.has(k - 4):
                        pool.wait_ge(s["g_sd"], r.done(k - 4))
                    for i in range(2):
                        last = pool.tensor_tensor(prod[:, i, :], th[:, (k - 3) % 2, :], vec[:, 2 + i, :], ALU.mult)
                    last.then_inc(s["g_prod"], 1)
                if r.has(k - 2):
                    layernorm(r, "g", 1, k - 2)
                if r.has(k - 3):
                    score_parts(r, k - 3)
                if r.has(k + 1):
                    g = k + 1
                    hold(pool, adj_in[g // HALF_SLOTS % 2], r.dma(g))
                    if r.has(g - 2):
                        hold(pool, s["s_biased"], r.done(g - 2))
                    pool.tensor_scalar(neg_bias[:, g % 2, :], adj8[:, g % SLOTS, :], -1.0, -NEG, ALU.add, ALU.mult
                                       ).then_inc(s["bias_mask"], 1)
                if r.has(k - 3):
                    g = k - 3
                    if r.has(g - 2):
                        hold(pool, s["z_masked"], r.done(g - 2))
                    pool.tensor_scalar(no_edge[:, g % 2, :], adj8[:, g % SLOTS, :], -1.0, 1.0, ALU.mult, ALU.add)
                    pool.tensor_scalar(floor[:, g % 2, :], adj8[:, g % SLOTS, :], LEAST, NO_EDGE, ALU.mult, ALU.add
                                       ).then_inc(s["masks"], 1)
                if r.has(k + 5):
                    layernorm(r, "m", 0, k + 5)

            with pool.Fori(0, PAIRS) as p:
                one = pool.snap(p + 1)

                def start(r, k):
                    if k == 2:
                        hold(pool, s["out_bias"], one)

                run_steps(pool, p, step, start, dma=True)

        @block.scalar
        def _(act):
            def normed(r, kind, i, g, src, dst):
                act.wait_ge(s[kind + "_shift"], r.done(g))
                act.activation(dst, src, ACT.Relu, bias=shift[:, i, g % SLOTS:g % SLOTS + 1],
                               scale=rstd[:, i, g % SLOTS:g % SLOTS + 1]).then_inc(s[kind + "_h"], 1)

            def queries_keys(r, k, i):
                if not r.has(k + 2):
                    return
                g = k + 2 - k % 2
                c = QK_ORDER[k % 2 * 3 + i]
                q = c < KC
                act.wait_ge(s[f"qk_ps{i}"], r.done(k + 2))
                act.activation(QKT[:, c, g % 4 * N:(g % 4 + 2) * N], bank(7 if i == 2 else 6)[:, 0:2 * N], ACT.Identity,
                               bias=q_bias8[:, c:c + 1] if q else cols[:, c:c + 1],
                               scale=MD ** -0.5 if q else 1.0).then_inc(s[f"qk{i}"], 1)

            def step(r, k):
                if r.has(k - 3):
                    act.wait_ge(s["g_hT"], r.done(k - 3))
                    act.activation(gT_hi[:], chunks(bank(7)), ACT.Copy).then_inc(s["g_hi"], 1)
                if r.has(k - 1):
                    act.wait_ge(s["pt_ps"], r.done(k - 1))
                    act.activation(PTA[:].rearrange("p (e n) -> p e n", e=2), banks(3, 2)[:, :, 0:D], ACT.Copy).then_inc(s["pt"], 1)
                if r.has(k - 5):
                    act.wait_ge(s["z_shifted"], r.done(k - 5))
                    act.activation(LG[:, (k - 5) % 2, :], LG[:, (k - 5) % 2, :], ACT.Exp).then_inc(s["z_exp"], 1)
                queries_keys(r, k, 0)
                if r.has(k - 6):
                    act.wait_ge(s["y_min"], r.done(k - 6))
                    act.activation(ey[:], ey[:], ACT.Exp).then_inc(s["y_exp"], 1)
                if r.has(k - 3):
                    act.wait_ge(s["g_h_ps"], r.done(k - 3))
                    if r.has(k - 5):
                        act.wait_ge(s["g_prod"], r.done(k - 5))
                    act.activation(th[:, (k - 3) % 2, :], bank(7)[:, 0:D], ACT.Tanh).then_inc(s["g_th"], 1)
                if r.has(k - 2):
                    act.wait_ge(s["cT_ps"], r.done(k - 2))
                    act.activation(cT_hi[:], chunks(bank(6)), ACT.Copy).then_inc(s["cT_hi"], 1)
                if r.has(k - 5):
                    for q in range(2):
                        act.wait_ge(s[f"gpt_ps{q}"], r.done(k - 5))
                        act.activation(PTG[:, q, :], bank(3 + q), ACT.Copy).then_inc(s[f"gpt{q}"], 1)
                if r.has(k):
                    act.wait_ge(s["s_shifted"], r.done(k))
                    act.activation(LA[:, k % 2, :], LA[:, k % 2, :], ACT.Exp).then_inc(s["s_exp"], 1)
                if r.has(k - 3):
                    act.wait_ge(s["g_gate_ps"], r.done(k - 3))
                    if r.has(k - 7):
                        act.wait_ge(s["mixed"], r.done(k - 7))
                    act.activation(gate[:, (k - 3) % 4, :], bank(7)[:, 0:D], ACT.Tanh, scale=0.5).then_inc(s["g_gate"], 1)
                if r.has(k - 5):
                    act.wait_ge(s["gpt_ps2"], r.done(k - 5))
                    act.activation(PTG[:, 2, :], bank(3), ACT.Copy).then_inc(s["gpt2"], 1)
                if r.has(k - 4):
                    act.wait_ge(s["g_sdT_ps"], r.done(k - 4))
                    act.activation(sdT[:, k % 2, :], sdT_ps, ACT.Copy).then_inc(s["g_sdT"], 1)
                if r.has(k + 4):
                    act.wait_ge(s["m_hT"], r.done(k + 4))
                    act.activation(hT_hi[:, :, k % 4, :], chunks(bank(7)), ACT.Copy).then_inc(s["m_hi"], 1)
                if r.has(k - 4):
                    act.wait_ge(s["z_ps"], r.done(k - 4))
                    act.activation(LG[:, k % 2, :].rearrange("p (e n) -> p e n", e=3), banks(0, 3),
                                   ACT.Copy, scale=SLOPE).then_inc(s["z_slope"], 1)
                if r.has(k + 2):
                    act.wait_ge(s["m_v"], r.done(k + 2))
                    act.activation(vaug[:, (k + 2) % 4, :, 0:MD], bank(7)[:, 0:D].rearrange("p (h d) -> p h d", h=MH),
                                   ACT.Copy).then_inc(s["m_vaug"], 1)
                if r.has(k - 2):
                    normed(r, "g", 1, k - 2, x1[:, (k - 2) % SLOTS, :], hG[:, (k - 2) % SLOTS, :])
                if r.has(k + 5):
                    normed(r, "m", 0, k + 5, xin[:, (k + 5) % SLOTS, :], hM[:])
                queries_keys(r, k, 1)
                queries_keys(r, k, 2)

            with act.Fori(0, PAIRS) as p:
                v_in = act.snap(p * 48 + 48)
                one = act.snap(p + 1)
                w_ins = [act.snap(p * 48 + 16 * (n + 1)) for n in range(3)]
                for n, hi in enumerate((qk_hi, qk_hi, vf_hi, vf_hi, hg_hi, hg_hi)):
                    act.wait_ge(w_in[n % 2], w_ins[n // 2])
                    act.activation(hi[:, :, n % 2 * D:(n % 2 + 1) * D], stages[n % 2], ACT.Copy).then_inc(s["w_hi"], 1)
                act.wait_ge(s["v_in"], v_in)
                act.activation(q_bias8[:], cols[:, 0:KC], ACT.Copy, scale=MD ** -0.5).then_inc(s["setup_act"], 1)
                act.wait_ge(s["setup_act"], one)
                run_steps(act, p, step)

        @block.vector
        def _(dve):
            dve.wait_ge(s["const_in"], 48)
            for i, sel in enumerate((sel_s, sel_d)):
                dve.tensor_copy(sel[:].rearrange("c a n -> c (a n)"), LG[0:PARTS * SD, i, :]).then_inc(s["setup_dve"], 1)
            dve.tensor_copy(idb[:], idf[:])
            dve.tensor_scalar(far_id[:], idf[:], -FAR, None, ALU.mult).then_inc(s["setup_dve"], 1)

            def statistics(r, kind, i, g, src):
                b = g % SLOTS
                dve.bn_stats(stats[:, i, b, :], src[:, b, :]).then_inc(s[kind + "_stats"], 1)
                hold(dve, s[kind + "_stats"], r.done(g))
                dve.bn_aggr(mv[:, i, b, :], stats[:, i, b, :]).then_inc(s[kind + "_mv"], 1)

            def attention_scores(r, g):
                Sb = LA[:, g % 2, :].rearrange("p (h n) -> p h n", h=MH)
                dve.wait_ge(s["s_ps"], r.done(g))
                dve.wait_ge(s["bias_mask"], r.done(g))
                dve.tensor_tensor(LA[:, g % 2, :].rearrange("p (e h n) -> p e h n", e=2, h=KC),
                                  banks(0, 2)[:, :, 0:D].rearrange("p e (h n) -> p e h n", h=KC),
                                  neg_bias[:, g % 2, :].unsqueeze(1).unsqueeze(1).broadcast_to([128, 2, KC, N]),
                                  ALU.add).then_inc(s["s_biased"], 1)
                dve.wait_ge(s["s_biased"], r.done(g))
                dve.tensor_reduce(mx[:, 0, 0:MH], Sb, AX.X, ALU.max).then_inc(s["s_max"], 1)
                dve.wait_ge(s["s_max"], r.done(g))
                dve.tensor_tensor(Sb, Sb, mx[:, 0, 0:MH].unsqueeze(2).broadcast_to([128, MH, N]),
                                  ALU.subtract).then_inc(s["s_shifted"], 1)

            def gated(r, g):
                b = g % SLOTS
                dve.wait_ge(s["y_exp"], r.done(g))
                dve.scalar_tensor_tensor(y[:], y[:], 0.0, ey[:], ALU.max, ALU.add).then_inc(s["elu"], 1)
                dve.wait_ge(s["elu"], r.done(g))
                dve.scalar_tensor_tensor(y[:], y[:], -1.0, hG[:, b, :], ALU.add, ALU.subtract).then_inc(s["elu_f"], 1)
                dve.wait_ge(s["elu_f"], r.done(g))
                dve.wait_ge(s["g_gate"], r.done(g))
                dve.scalar_tensor_tensor(y[:], gate[:, g % 4, :], 1.0, y[:], ALU.add, ALU.mult).then_inc(s["mixed"], 1)
                dve.wait_ge(s["mixed"], r.done(g))
                dve.wait_ge(s["xf"], r.done(g))
                dve.scalar_tensor_tensor(x1[:, b, :], y[:], 0.5, x1[:, b, :], ALU.mult, ALU.add).then_inc(s["x2"], 1)

            def step(r, k):
                if r.has(k - 3):
                    dve.wait_ge(s["g_hi"], r.done(k - 3))
                    dve.tensor_tensor(gT_lo[:], chunks(bank(7)), gT_hi[:].bitcast(F32), ALU.subtract).then_inc(s["g_lo"], 1)
                if r.has(k):
                    attention_scores(r, k)
                if r.has(k - 1):
                    c_ps = bank(5)[:, 0:MH * (MD + 1)].rearrange("p (h d) -> p h d", h=MH)
                    dve.wait_ge(s["c_ps"], r.done(k - 1))
                    dve.reciprocal(rden[:, 0, 0:MH].unsqueeze(2), c_ps[:, :, MD:MD + 1]).then_inc(s["c_rden"], 1)
                    dve.wait_ge(s["c_rden"], r.done(k - 1))
                    dve.tensor_tensor(ctxn[:, (k - 1) % 2, :].rearrange("p (h d) -> p h d", h=MH), c_ps[:, :, 0:MD],
                                      rden[:, 0, 0:MH].unsqueeze(2).broadcast_to([128, MH, MD]),
                                      ALU.mult).then_inc(s["c_norm"], 1)
                if r.has(k - 3):
                    dve.wait_ge(s["g_th"], r.done(k - 3))
                    dve.tensor_tensor(haug[:, (k - 3) % 4, :, 0:GD], bank(7)[:, 0:D].rearrange("p (a e) -> p a e", a=GH),
                                      bg_bc.rearrange("p (a e) -> p a e", a=GH), ALU.add).then_inc(s["g_haug"], 1)
                if r.has(k - 2):
                    dve.wait_ge(s["cT_hi"], r.done(k - 2))
                    dve.tensor_tensor(cT_lo[:], chunks(bank(6)), cT_hi[:].bitcast(F32), ALU.subtract).then_inc(s["cT_lo"], 1)
                if r.has(k - 6):
                    gated(r, k - 6)
                if r.has(k - 3):
                    dve.wait_ge(s["g_prod"], r.done(k - 3))
                    dve.tensor_reduce(sd[:, (k - 3) % 4, :], prod[:].rearrange("p k (a e) -> p (k a) e", a=GH), AX.X,
                                      ALU.add).then_inc(s["g_sd"], 1)
                if r.has(k - 2):
                    b = (k - 2) % SLOTS
                    dve.wait_ge(s["o_ps"], r.done(k - 2))
                    dve.wait_ge(s["xb"], r.done(k - 2))
                    dve.tensor_tensor(x1[:, b, :], bank(6)[:, 0:D], x1[:, b, :], ALU.add).then_inc(s["x1"], 1)
                    dve.wait_ge(s["x1"], r.done(k - 2))
                    statistics(r, "g", 1, k - 2, x1)
                if r.has(k + 4):
                    dve.wait_ge(s["m_hi"], r.done(k + 4))
                    dve.tensor_tensor(hT_lo[:, :, k % 4, :], chunks(bank(7)), hT_hi[:, :, k % 4, :].bitcast(F32),
                                      ALU.subtract).then_inc(s["m_lo"], 1)
                if r.has(k + 5):
                    dve.wait_ge(x_in[(k + 5) % SLOTS], r.dma(k + 5))
                    statistics(r, "m", 0, k + 5, xin)
                if r.has(k - 4):
                    Lk = LG[:, k % 2, :].rearrange("p (a n) -> p a n", a=GH)
                    L3 = LG[:, k % 2, :].rearrange("p (e n) -> p e n", e=3)
                    dve.wait_ge(s["z_slope"], r.done(k - 4))
                    dve.tensor_tensor(L3, banks(0, 3), L3, ALU.max).then_inc(s["z_leaky"], 1)
                    dve.wait_ge(s["z_leaky"], r.done(k - 4))
                    dve.wait_ge(s["masks"], r.done(k - 4))
                    dve.tensor_tensor(Lk, Lk, floor[:, k % 2, :].unsqueeze(1).broadcast_to([128, GH, N]),
                                      ALU.max).then_inc(s["z_masked"], 1)
                if r.has(k - 5):
                    pv = bank(5)[:, 0:GH * (GD + 1)].rearrange("p (a e) -> p a e", a=GH)
                    dve.wait_ge(s["pv_ps"], r.done(k - 5))
                    dve.reciprocal(rden[:, 1, :].unsqueeze(2), pv[:, :, GD:GD + 1]).then_inc(s["pv_rden"], 1)
                    dve.wait_ge(s["pv_rden"], r.done(k - 5))
                    dve.tensor_tensor(y[:].rearrange("p (a e) -> p a e", a=GH), pv[:, :, 0:GD],
                                      rden[:, 1, :].unsqueeze(2).broadcast_to([128, GH, GD]),
                                      ALU.mult).then_inc(s["pv_norm"], 1)
                if r.has(k - 4):
                    dve.wait_ge(s["z_masked"], r.done(k - 4))
                    dve.tensor_reduce(mx[:, 1, :], Lk, AX.X, ALU.max).then_inc(s["z_max"], 1)
                    dve.wait_ge(s["z_max"], r.done(k - 4))
                    dve.tensor_tensor(Lk, Lk, mx[:, 1, :].unsqueeze(2).broadcast_to([128, GH, N]),
                                      ALU.subtract).then_inc(s["z_shifted"], 1)

            with dve.Fori(0, PAIRS) as p:
                v_in = dve.snap(p * 48 + 48)
                one = dve.snap(p + 1)
                his = [dve.snap(p * 6 + n + 1) for n in range(6)]
                for n, (hi, lo) in enumerate(((qk_hi, qk_lo), (vf_hi, vf_lo), (hg_hi, hg_lo))):
                    for half in range(2):
                        cut = slice(half * D, (half + 1) * D)
                        dve.wait_ge(s["w_hi"], his[2 * n + half])
                        dve.tensor_tensor(lo[:, :, cut], stages[half], hi[:, :, cut].bitcast(F32), ALU.subtract
                                          ).then_inc(s["stage_split"], 1)
                dve.wait_ge(s["v_in"], v_in)
                dve.tensor_copy(bv_cols, cols[:, 2 * KC:3 * KC].unsqueeze(2).broadcast_to([128, KC, 128])).then_inc(s["bv_cols"], 1)
                hb = [dve.snap(p * 8 + k) for k in range(1, 9)]
                dve.tensor_copy(hb_part[:, 0, :], hb_row[:]).then_inc(s["hb_step"], 1)
                dve.wait_ge(s["hb_step"], hb[0])
                dve.tensor_tensor(hb_rest, hb_row[:], hb_part[:, 0, :], ALU.subtract).then_inc(s["hb_step"], 1)
                dve.wait_ge(s["hb_step"], hb[1])
                dve.tensor_copy(hb_part[:, 1, :], hb_rest).then_inc(s["hb_step"], 1)
                dve.wait_ge(s["hb_step"], hb[2])
                dve.tensor_tensor(hb_rest, hb_rest, hb_part[:, 1, :], ALU.subtract).then_inc(s["hb_step"], 1)
                dve.wait_ge(s["hb_step"], hb[3])
                dve.tensor_copy(hb_part[:, 2, :], hb_rest)
                dve.tensor_scalar(hb_acc, hb_part[:, 0, :], idf[0:PARTS, 0:1], None, ALU.mult).then_inc(s["hb_step"], 1)
                dve.wait_ge(s["hb_step"], hb[4])
                dve.scalar_tensor_tensor(hb_acc, hb_part[:, 1, :], idf[0:PARTS, 1:2], hb_acc, ALU.mult, ALU.add).then_inc(s["hb_step"], 1)
                dve.wait_ge(s["hb_step"], hb[5])
                dve.scalar_tensor_tensor(hb3[:], hb_part[:, 2, :], idf[0:PARTS, 2:3], hb_acc, ALU.mult, ALU.add).then_inc(s["hb_step"], 2)

                def start(r, k):
                    if k == 0:
                        dve.wait_ge(s["out_bias_ps"], one)
                        dve.tensor_tensor(out_bias, bank(5)[:, 0:D], out_bias, ALU.add).then_inc(s["out_bias"], 1)

                run_steps(dve, p, step, start, dma=True)

        @block.tensor
        def _(pe):
            pe.wait_ge(s["setup_dve"], 3)
            pe.wait_ge(s["setup_pool"], 1)

            def features(src, dst):
                for c in range(KC):
                    last = pe.transpose(dst[:, c * 128:(c + 1) * 128], src[:, c * 128:(c + 1) * 128], idf[:])
                return last

            def nodes_times(dst, hi, lo, w_hi, w_lo, at, begun=False):
                n = 0
                for a, w in ((hi, w_hi), (hi, w_lo), (lo, w_hi)):
                    for c in range(KC):
                        last = pe.matmul(dst, a(c), w[:, c, at:at + D], start=(n == 0 and not begun), stop=(n == 3 * KC - 1))
                        n += 1
                return last

            def queries_keys(r, k, i, *bank_users):
                if not r.has(k + 2):
                    return
                g = k + 2 - k % 2
                c = QK_ORDER[k % 2 * 3 + i]
                if i == 0:
                    pe.wait_ge(s["m_lo"], r.done(g + 1))
                wait_latest(pe, r, *bank_users)
                dst = bank(7 if i == 2 else 6)[:, 0:2 * N]
                m = 0
                for w, a in ((qk_hi, hT_hi), (qk_lo, hT_hi), (qk_hi, hT_lo)):
                    for j in range(KC):
                        last = pe.matmul(dst, w[:, j, c * 128:(c + 1) * 128],
                                         a[:, j, g % 4:g % 4 + 2, :].rearrange("p b n -> p (b n)"), start=(m == 0), stop=(m == 3 * KC - 1))
                        m += 1
                last.then_inc(s[f"qk_ps{i}"], 1)

            def graph_transposes(r, g, q):
                for a in range(4 * q, 4 * q + 4):
                    last = pe.transpose(bank(3 + q % 2)[:, (a % 4) * N:(a % 4 + 1) * N], LG[:, g % 2, a * N:(a + 1) * N], idf[:])
                last.then_inc(s[f"gpt_ps{q}"], 1)

            def step(r, k):
                if r.has(k):
                    if k % 2 == 0:
                        for i in range(3):
                            pe.wait_ge(s[f"qk{i}"], r.done(k + 1))
                    wait_latest(pe, r, ("z_leaky", k - 5), ("s_biased", k - 1))
                    for i in range(MH):
                        h = head_of(i)
                        rows = slice(64 * (h % 2), 64 * (h % 2) + 64)
                        at = slice(k % 4 * N, (k % 4 + 1) * N)
                        last = pe.matmul(bank(i // KC)[:, (i % KC) * N:(i % KC + 1) * N],
                                         QKT[rows, h // 2, at], QKT[rows, KC + h // 2, at], start=True, stop=True)
                    last.then_inc(s["s_ps"], 1)
                if r.has(k - 3):
                    pe.wait_ge(s["g_h"], r.done(k - 3))
                    wait_latest(pe, r, ("qk2", k + 1), ("g_gate", k - 4))
                    features(hG[:, (k - 3) % SLOTS, :], bank(7)).then_inc(s["g_hT"], 1)
                if r.has(k - 1):
                    pe.wait_ge(s["s_exp"], r.done(k - 1))
                    wait_latest(pe, r, ("gpt2", k - 6), ("pt", k - 2))
                    for i in range(MH):
                        last = pe.transpose(bank(3 + i // KC)[:, (i % KC) * N:(i % KC + 1) * N],
                                            LA[:, (k - 1) % 2, i * N:(i + 1) * N], idf[:])
                    last.then_inc(s["pt_ps"], 1)
                queries_keys(r, k, 0, ("qk1", k + 1))
                if r.has(k - 1):
                    pe.wait_ge(s["pt"], r.done(k - 1))
                    pe.wait_ge(s["m_vaug"], r.done(k - 1))
                    wait_latest(pe, r, ("pv_norm", k - 6), ("g_sdT", k - 5), ("c_norm", k - 2))
                    for i in range(MH):
                        h = head_of(i)
                        last = pe.matmul(bank(5)[:, h * (MD + 1):(h + 1) * (MD + 1)], PTA[:, i * N:(i + 1) * N],
                                         vaug[:, (k - 1) % 4, h, :], start=True, stop=True)
                    last.then_inc(s["c_ps"], 1)
                g_hi, g_lo = (lambda c: gT_hi[:, c, :]), (lambda c: gT_lo[:, c, :])
                if r.has(k - 3):
                    pe.wait_ge(s["g_lo"], r.done(k - 3))
                    nodes_times(bank(7)[:, 0:D], g_hi, g_lo, hg_hi, hg_lo, 0).then_inc(s["g_h_ps"], 1)
                if r.has(k - 2):
                    pe.wait_ge(s["c_norm"], r.done(k - 2))
                    wait_latest(pe, r, ("qk0", k + 2), ("x1", k - 3))
                    features(ctxn[:, k % 2, :], bank(6)).then_inc(s["cT_ps"], 1)
                if r.has(k - 5):
                    pe.wait_ge(s["z_exp"], r.done(k - 5))
                    wait_latest(pe, r, ("pt", k - 1), ("gpt2", k - 6))
                    graph_transposes(r, k - 5, 0)
                    graph_transposes(r, k - 5, 1)
                if r.has(k - 3):
                    pe.wait_ge(s["g_haug"], r.done(k - 3))
                    pe.matmul(bank(7)[:, 0:D], ones3[:], hb3[:], start=True, stop=False)
                    nodes_times(bank(7)[:, 0:D], g_hi, g_lo, hg_hi, hg_lo, D, begun=True).then_inc(s["g_gate_ps"], 1)
                if r.has(k - 5):
                    pe.wait_ge(s["gpt0"], r.done(k - 5))
                    graph_transposes(r, k - 5, 2)
                if r.has(k - 4):
                    pe.wait_ge(s["g_sd3"], r.done(k - 4))
                    wait_latest(pe, r, ("c_norm", k - 1), ("pv_norm", k - 6), ("g_sdT", k - 5))
                    pe.transpose(sdT_ps, sd3[:, k % 4, :, :].rearrange("p a n -> p (a n)"), idb[:]).then_inc(s["g_sdT_ps"], 1)
                if r.has(k - 2):
                    pe.wait_ge(s["cT_lo"], r.done(k - 2))
                    nodes_times(bank(6)[:, 0:D], lambda c: cT_hi[:, c, :], lambda c: cT_lo[:, c, :], vf_hi, vf_lo, D
                                ).then_inc(s["o_ps"], 1)
                if r.has(k + 4):
                    pe.wait_ge(s["m_h"], r.done(k + 4))
                    wait_latest(pe, r, ("g_gate", k - 3), ("qk2", k + 1), ("m_lo", k + 3))
                    features(hM, bank(7)).then_inc(s["m_hT"], 1)
                if r.has(k - 4):
                    pe.wait_ge(s["masks"], r.done(k - 4))
                    pe.wait_ge(s["g_sdT"], r.done(k - 4))
                    wait_latest(pe, r, ("s_biased", k), ("z_leaky", k - 5))
                    for q in range(QUADS):
                        four = bank(q).rearrange("p (a n) -> p a n", a=4)
                        pe.matmul(four, sdT[:, k % 2, :], sel_s[:, 4 * q:4 * q + 4, :], start=True, stop=False)
                        for a in range(4):
                            pe.matmul(four[:, a, :], sel_d[:, 4 * q + a, :], sdT[:, k % 2, :], start=False, stop=False)
                        last = pe.matmul(four, far_id[:], no_edge[:, k % 2, :].unsqueeze(1).broadcast_to([128, 4, N]),
                                         start=False, stop=True)
                    last.then_inc(s["z_ps"], 1)
                if r.has(k + 2):
                    wait_latest(pe, r, ("m_lo", k + 4), ("g_gate", k - 3))
                    b = (k + 2) % 4
                    nodes_times(bank(7)[:, 0:D], lambda c: hT_hi[:, c, b, :], lambda c: hT_lo[:, c, b, :], vf_hi, vf_lo, 0
                                ).then_inc(s["m_v"], 1)
                if r.has(k - 5):
                    wait_latest(pe, r, ("g_sdT", k - 4), ("pv_norm", k - 6))
                    for q in range(QUADS):
                        pe.wait_ge(s[f"gpt{q}"], r.done(k - 5))
                        for a in range(4 * q, 4 * q + 4):
                            last = pe.matmul(bank(5)[:, a * (GD + 1):(a + 1) * (GD + 1)], PTG[:, q, (a % 4) * N:(a % 4 + 1) * N],
                                             haug[:, (k - 5) % 4, a, :], start=True, stop=True)
                    last.then_inc(s["pv_ps"], 1)
                queries_keys(r, k, 1, ("x1", k - 2), ("qk0", k + 2))
                queries_keys(r, k, 2, ("m_vaug", k + 2))

            with pe.Fori(0, PAIRS) as p:
                qk_split, vf_split, all_split = (pe.snap(p * 6 + n) for n in (2, 4, 6))
                hb_done = pe.snap(p * 8 + 8)
                one = pe.snap(p + 1)

                def start(r, k):
                    if k == -2:
                        hold(pe, s["stage_split"], qk_split)
                        hold(pe, s["stage_split"], vf_split)
                    if k == 0:
                        pe.wait_ge(s["bv_cols"], one)
                        for c in range(KC):
                            for w in (vf_hi, vf_lo):
                                last = pe.matmul(bank(5)[:, 0:D], bv_cols[:, c, :], w[:, c, D:2 * D].bitcast(F32),
                                                 start=(c == 0 and w is vf_hi), stop=(c == KC - 1 and w is vf_lo))
                        last.then_inc(s["out_bias_ps"], 1)
                    if k == 1:
                        hold(pe, s["out_bias"], one)
                    if k == 3:
                        hold(pe, s["stage_split"], all_split)
                        hold(pe, s["hb_step"], hb_done)

                hold(pe, s["stage_split"], qk_split)
                run_steps(pe, p, step, start)


def kernel(**inputs):
    import numpy as np
    import concourse.bacc as bacc
    from concourse.bass_utils import run_bass_kernel_spmd as run

    def of(layer, name):
        return np.asarray(inputs[f"L{layer}_gnn_{name}"])

    w_qk = np.stack([np.concatenate([of(m, "Wq"), of(m, "Wk")], 1) for m in (0, 2)])
    w_vf = np.stack([np.concatenate([of(m, "Wv"), of(m, "Wf")], 1) for m in (0, 2)])
    w_hg = np.stack([np.concatenate([of(g, "W").transpose(1, 0, 2).reshape(D, D), of(g, "H_w").T], 1) for g in (1, 3)])
    b_cols = np.stack([np.concatenate([of(m, "bq"), of(m, "bk"), of(m, "bv")]).reshape(3 * KC, 128).T for m in (0, 2)])
    vecs = np.stack([np.stack([of(g - 1, "bf"), np.tile(of(g, "b"), GH),
                               of(g, "w_src").reshape(D), of(g, "w_dst").reshape(D)]) for g in (1, 3)])
    h_b = np.stack([of(g, "H_b") for g in (1, 3)])
    row = np.arange(PARTS * SD)[:, None, None]
    head = np.arange(GH)[None, :, None]
    sel_src = np.broadcast_to(row % SD == head, (PARTS * SD, GH, 128)).astype(np.float32).reshape(PARTS * SD, GH * 128)
    sel_dst = np.broadcast_to(row % SD == GH + head, (PARTS * SD, GH, 128)).astype(np.float32).reshape(PARTS * SD, GH * 128)
    arrays = {
        "x": np.asarray(inputs["x"]), "adj": np.asarray(inputs["adj"]), "w_qk": w_qk, "w_vf": w_vf, "w_hg": w_hg,
        "b_cols": b_cols, "vecs": vecs, "h_b": h_b, "ident": np.eye(128, dtype=np.float32), "sel_src": sel_src, "sel_dst": sel_dst,
    }
    nc = bacc.Bacc("TRN2", target_bir_lowering=False, num_devices=1)
    args = []
    for name, a in arrays.items():
        arrays[name] = a = np.ascontiguousarray(a)
        args.append(nc.dram_tensor(name, a.shape, mybir.dt.from_np(a.dtype), kind="ExternalInput").ap())
    args.append(nc.dram_tensor("out", inputs["x"].shape, F32, kind="ExternalOutput").ap())
    graph_stack(nc, *args)
    r = run(nc, [arrays], core_ids=[0])
    return r.results[0]["out"]
```

```python
from contextlib import ExitStack

import concourse.bass as bass
from concourse import mybir

F32 = mybir.dt.float32
F32R = mybir.dt.float32r
BF16 = mybir.dt.bfloat16
U8 = mybir.dt.uint8
ALU = mybir.AluOpType
ACT = mybir.ActivationFunctionType
AX = mybir.AxisListType

SLOTS = 8
PAIRS = 2
N = 128
D = 384
KC = D // 128
MH, MD = 6, 64
GH, GD = 12, 32
QUADS = GH // 4
NEG = -9000000000000000.0
NO_EDGE = -999.0
SLOPE = 0.2
FAR = float(2.0**126)
LEAST = -3.0e38
EPS = 1e-5
PARTS = 3
SD = 2 * GH
HALF_SLOTS = SLOTS // 2
QK_ORDER = [0, 3, 1, 4, 2, 5]

FIRST_STEP, STEPS_BEHIND = -5, 6


def graph_stack(nc, x, adj, w_qk, w_vf, w_hg, b_cols, vecs, h_b, ident, sel_src, sel_dst, out):
    B = x.shape[0]
    ALL = PAIRS * B

    with ExitStack() as ctx:
        def sb(name, shape, dt=F32):
            return ctx.enter_context(nc.sbuf_tensor(name, shape, dt))

        def sem(name):
            return ctx.enter_context(nc.semaphore(name))

        x_mid = nc.dram_tensor("x_mid", x.shape, F32, kind="Internal").ap()

        qk_hi, qk_lo = sb("qk_hi", [128, KC, 2 * D], F32R), sb("qk_lo", [128, KC, 2 * D], F32R)
        vf_hi, vf_lo = sb("vf_hi", [128, KC, 2 * D], F32R), sb("vf_lo", [128, KC, 2 * D], F32R)
        hg_hi, hg_lo = sb("hg_hi", [128, KC, 2 * D], F32R), sb("hg_lo", [128, KC, 2 * D], F32R)
        vec = sb("vec", [128, PAIRS, 4, D])
        cols = sb("cols", [128, PAIRS, 3 * KC])
        q_bias8 = sb("q_bias8", [128, PAIRS, KC])
        hb3 = sb("hb3", [PARTS, PAIRS, D], BF16)
        stage = sb("stage", [128, 2, KC, D // 2])

        idf = sb("idf", [128, 128])
        idb = sb("idb", [128, 128], BF16)
        far_id = sb("far_id", [128, 128], BF16)
        ones3 = sb("ones3", [PARTS, 128], BF16)
        sel_s = sb("sel_s", [PARTS * SD, GH], BF16)
        sel_d = sb("sel_d", [PARTS * SD, GH], BF16)
        minus_half = sb("minus_half", [128, 1])

        adj8 = sb("adj8", [128, SLOTS, N], U8)
        neg_bias = sb("neg_bias", [128, 2, N])
        floor = sb("floor", [128, 2, N])
        no_edge = sb("no_edge", [128, 2, N], BF16)
        xin = sb("xin", [128, SLOTS, D])
        x1 = sb("x1", [128, SLOTS, D])
        hM = sb("hM", [128, D])
        hG = sb("hG", [128, SLOTS, D])
        stats = sb("stats", [128, 2, SLOTS, 6])
        mv = sb("mv", [128, 2, SLOTS, 2])
        var_eps = sb("var_eps", [128, 2, SLOTS])
        rstd = sb("rstd", [128, 2, SLOTS])
        shift = sb("shift", [128, 2, SLOTS])
        hT_hi = sb("hT_hi", [128, KC, 4, N], F32R)
        hT_lo = sb("hT_lo", [128, KC, 4, N], F32R)
        gT_hi = sb("gT_hi", [128, KC, N], F32R)
        gT_lo = sb("gT_lo", [128, KC, N], F32R)
        QKT = sb("QKT", [128, 2 * KC, 4 * N])
        th = sb("th", [128, 2, D])
        gate = sb("gate", [128, 4, D])
        vaug = sb("vaug", [128, 4, MH, MD + 1])
        haug = sb("haug", [128, 4, GH, GD + 1])
        LA = sb("LA", [128, 2, MH * N])
        LG = sb("LG", [128, 2, GH * N])
        PTA = sb("PTA", [128, MH * N])
        PTG = sb("PTG", [128, QUADS, 4 * N])
        neg_max = sb("neg_max", [128, 2, GH])
        rden = sb("rden", [128, 2, GH])
        ctxn = sb("ctxn", [128, 2, D])
        cT_hi = sb("cT_hi", [128, KC, N], F32R)
        cT_lo = sb("cT_lo", [128, KC, N], F32R)
        prod = sb("prod", [128, 2, D])
        sd = sb("sd", [128, 4, SD])
        sd_rest = sb("sd_rest", [128, 4, 2, SD])
        sd3 = sb("sd3", [128, 4, PARTS, SD], BF16)
        sdT = sb("sdT", [PARTS * SD, 2, N], BF16)
        y = sb("y", [128, D])
        ey = sb("ey", [128, D])
        sel_stage = x1[0:PARTS * SD, 0:2, 0:GH]
        wf_stage = [LG[:, 0, 0:KC * D].rearrange("p (c n) -> p c n", c=KC),
                    LA[:].rearrange("p a n -> p (a n)")[:, 0:KC * D].rearrange("p (c n) -> p c n", c=KC)]
        bv_cols = [LG[:, 1, i * D:(i + 1) * D].rearrange("p (c n) -> p c n", c=KC) for i in range(PAIRS)]
        hb_row, hb_rest, hb_acc = hG[0:PARTS, 0:2, :], hG[0:PARTS, 2, :], hG[0:PARTS, 3, :]
        hb_part = hG[0:PARTS, 4:6, :].rearrange("p a n -> p (a n)").bitcast(BF16).rearrange("p (k n) -> p k n", k=4)

        COLS = D // 2
        PIECES = [(w, hi[:, :, at:at + COLS], lo[:, :, at:at + COLS], at)
                  for w, hi, lo in ((w_qk, qk_hi, qk_lo), (w_vf, vf_hi, vf_lo), (w_hg, hg_hi, hg_lo)) for at in range(0, 2 * D, COLS)]
        CHANGES = {-2: range(0, 6), 2: range(6, 8), 3: range(8, 12)}

        psum = ctx.enter_context(nc.psum_tensor("psum", [128, 8, 512], F32))
        sdT_ps = psum[0:PARTS * SD, 5, 512 - N // 2:512].bitcast(BF16)

        def bank(i):
            return psum[:, i, :]

        def banks(i, k):
            return psum[:, i:i + k, :]

        def chunks(ap):
            return ap[:, 0:D].rearrange("p (c n) -> p c n", c=KC)

        s = {n: sem(n) for n in (
            "v_in", "const_in", "wf_in", "w_split", "setup_dve", "setup_act",
            "setup_pool", "hb_step", "w_hi", "bv_cols", "out_bias_ps", "out_bias", "bias_mask", "masks", "xb",
            "m_stats", "m_mv", "m_var", "m_rstd", "m_shift", "m_h", "m_hT", "m_hi", "m_lo", "m_v", "m_vaug",
            "qk_ps0", "qk_ps1", "qk_ps2", "qk0", "qk1", "qk2",
            "s_ps", "s_biased", "s_max", "s_exp", "pt_ps", "pt", "c_ps", "c_rden", "c_norm",
            "cT_ps", "cT_hi", "cT_lo", "o_ps", "x1",
            "g_stats", "g_mv", "g_var", "g_rstd", "g_shift", "g_h", "g_hT", "g_hi", "g_lo", "g_h_ps", "g_gate_ps",
            "g_th", "g_gate", "g_sigmoid", "g_haug", "g_prod", "g_sd", "g_sd_hi", "g_rest1", "g_sd_mid", "g_rest2", "g_sd3",
            "g_sdT_ps", "g_sdT", "z_ps", "z_slope", "z_leaky", "z_masked", "z_max", "z_shifted", "z_exp",
            "gpt_ps0", "gpt_ps1", "gpt_ps2", "gpt0", "gpt1", "gpt2",
            "pv_ps", "pv_rden", "pv_norm", "y_min", "y_exp", "ey_f", "xf", "elu_f", "mixed", "x2")}
        x_in = [sem(f"x_in{i}") for i in range(SLOTS)]
        stored = [sem(f"stored{i}") for i in range(SLOTS)]
        adj_in = [sem(f"adj_in{i}") for i in range(2)]
        w_in = [sem(f"w_in{i}") for i in range(2)]

        class Steps:

            def __init__(self, eng, base, lowest=None, highest=None, border=None, dma=None):
                snap = (lambda value: value) if isinstance(base, int) else eng.snap
                lo = -STEPS_BEHIND if lowest is None else 1
                hi = SLOTS + 5 if highest is None else highest + 1
                self.counts = {c: snap(base + c) for c in range(lo, hi + 1)}
                self.lowest, self.highest, self.border = lowest, highest, border
                if dma is not None:
                    self.dmas = {v: snap(dma * 16 + 16 * (v + 1))
                                 for v in range(-1 if lowest is None else 0, 2 if highest is None else 1)}

            def pair(self, g):
                return int(g >= self.border)

            def has(self, g):
                return (self.lowest is None or g >= self.lowest) and (self.highest is None or g <= self.highest)

            def done(self, g):
                return self.counts[g + 1]

            def dma(self, g):
                return self.dmas[g // SLOTS]

        def hold(eng, semaphore, value):
            eng.wait_ge(semaphore, value)
            eng.nop(nofuse=True)

        def wait_latest(eng, r, *users):
            for name, g in users:
                if r.has(g):
                    eng.wait_ge(s[name], r.done(g))
                    return

        def head_of(i):
            return 2 * (i % KC) + i // KC

        FAR_OFF = 2 * B

        def run_steps(eng, step, change, dma=False):
            visits = B // SLOTS
            for k in range(FIRST_STEP, SLOTS):
                if k in CHANGES:
                    change(0, k)
                step(Steps(eng, 0, 0, None, B, 0 if dma else None), k)
            with eng.Fori(1, visits - 1) as g:
                r = Steps(eng, g * SLOTS, border=FAR_OFF, dma=g if dma else None)
                for k in range(SLOTS):
                    step(r, k)
            for visit in (visits - 1, visits):
                r = Steps(eng, visit * SLOTS, border=B - visit * SLOTS, dma=visit if dma else None)
                for k in range(SLOTS):
                    if visit * SLOTS + k - B in CHANGES:
                        change(1, visit * SLOTS + k - B)
                    step(r, k)
            with eng.Fori(visits + 1, 2 * visits - 1) as g:
                r = Steps(eng, g * SLOTS, border=-FAR_OFF, dma=g if dma else None)
                for k in range(SLOTS):
                    step(r, k)
            r = Steps(eng, ALL - SLOTS, highest=SLOTS - 1, border=-FAR_OFF, dma=2 * visits - 1 if dma else None)
            for k in range(SLOTS + STEPS_BEHIND):
                step(r, k)

        def split_count(pair, k):
            return pair * len(PIECES) + CHANGES[k][-1] + 1

        block = ctx.enter_context(nc.Block())

        @block.sync
        def _(sp):
            for i in range(SLOTS):
                sp.sem_inc(stored[i], 16)

            def load_x(src, g, slot):
                sp.dma_start(xin[:, slot:slot + 1, :], src[bass.ds(g, 1), :, :].rearrange("b p n -> p b n")).then_inc(x_in[slot], 16)

            def load_adj(g, half):
                sp.dma_start(adj8[:, half * HALF_SLOTS:(half + 1) * HALF_SLOTS, :],
                             adj[bass.ds(g, HALF_SLOTS), :, :].rearrange("b p n -> p b n")).then_inc(adj_in[half], 16)

            def load_piece(n):
                w, hi, lo, at = PIECES[n % len(PIECES)]
                if n >= 2:
                    sp.wait_ge(s["w_split"], n - 1)
                sp.dma_start(stage[:, n % 2, :, :], w[n // len(PIECES)][:, at:at + COLS].rearrange("(c p) n -> p c n", p=128)
                             ).then_inc(w_in[n % 2], 16)

            load_x(x, 0, 0)
            for src, sel in ((ident, idf), (sel_src, sel_stage[:, 0, :]), (sel_dst, sel_stage[:, 1, :])):
                sp.dma_start(sel[:] if src is ident else sel, src).then_inc(s["const_in"], 16)
            load_x(x, 1, 1)
            for n in range(2):
                load_piece(n)
            for i in range(2, 4):
                load_x(x, i, i)
            for pair in range(PAIRS):
                sp.dma_start(cols[:, pair, :], b_cols[pair]).then_inc(s["v_in"], 16)
                sp.dma_start(vec[:, pair, :, :], vecs[pair].partition_broadcast(128)).then_inc(s["v_in"], 16)
                sp.dma_start(hb_row[:, pair, :], h_b[pair].partition_broadcast(PARTS)).then_inc(s["v_in"], 16)
                sp.dma_start(wf_stage[pair], w_vf[pair][:, D:2 * D].rearrange("(c p) n -> p c n", p=128)).then_inc(s["wf_in"], 16)
            load_adj(0, 0)
            for n in range(2, 6):
                load_piece(n)
            for i in range(4, SLOTS):
                load_x(x, i, i)
            load_adj(HALF_SLOTS, 1)
            for n in range(6, len(PIECES)):
                load_piece(n)

            def move(k, count, x_from, x_at, adj_at, to, to_at, filling=False):
                g = k + 6
                if x_from is not None:
                    hold(sp, s["xb"], count(k - 1))
                    load_x(x_from, x_at + g, g % SLOTS)
                g = k + 2
                if g % HALF_SLOTS == 0 and adj_at is not None and not (filling and k < 6):
                    hold(sp, s["masks"], count(k - 2))
                    load_adj(adj_at + g, g // HALF_SLOTS % 2)
                if to is not None:
                    hold(sp, s["x2"], count(k - 5))
                    slot = (k - 6) % SLOTS
                    sp.dma_start(to[bass.ds(to_at + k - 6, 1), :, :].rearrange("b p n -> p b n"), x1[:, slot:slot + 1, :]
                                 ).then_inc(stored[slot], 16)

            def loop(first, last, src, dst, offset):
                with sp.Fori(first, last) as g:
                    at = sp.snap(g * SLOTS - offset)
                    counts = {c: sp.snap(g * SLOTS + c) for c in range(-5, SLOTS)}
                    for k in range(SLOTS):
                        move(k, counts.get, src, at, at, dst, at)

            def straight(k):
                def of(g, first, second):
                    return (first, 0) if g < B else (second, -B)
                x_from, x_at = of(k + 6, x, x_mid) if 2 <= k < ALL - 6 else (None, 0)
                adj_at = (0 if k + 2 < B else -B) if k + 2 < ALL else None
                to, to_at = of(k - 6, x_mid, out) if k >= 6 else (None, 0)
                move(k, lambda c: c, x_from, x_at, adj_at, to, to_at, filling=k < 6)

            for k in range(SLOTS):
                straight(k)
            loop(1, B // SLOTS - 1, x, x_mid, 0)
            for k in range(B - SLOTS, B + SLOTS):
                ahead = {-8: range(0, 2), -2: range(2, 8), 2: range(8, 10), 3: range(10, 12)}
                for n in ahead.get(k - B, ()):
                    load_piece(len(PIECES) + n)
                straight(k)
            loop(B // SLOTS + 1, 2 * B // SLOTS - 1, x_mid, out, B)
            for k in range(ALL - SLOTS, ALL + STEPS_BEHIND):
                straight(k)
            for i in range(SLOTS):
                sp.wait_ge(stored[i], 16 * (ALL // SLOTS + 1))

        @block.gpsimd
        def _(pool):
            pool.memset(minus_half[:], -0.5)
            pool.memset(ones3[:], 1.0)
            pool.memset(vaug[:], 1.0)
            pool.memset(haug[:], 1.0).then_inc(s["setup_pool"], 1)
            pool.wait_ge(s["setup_pool"], 1)

            def layernorm(r, kind, i, g):
                b = g % SLOTS
                hold(pool, s[kind + "_mv"], r.done(g))
                pool.tensor_scalar(var_eps[:, i, b:b + 1], mv[:, i, b, 1:2], EPS, None, ALU.add).then_inc(s[kind + "_var"], 1)
                pool.wait_ge(s[kind + "_var"], r.done(g))
                pool.tensor_tensor(rstd[:, i, b:b + 1], var_eps[:, i, b:b + 1], minus_half[:], ALU.pow).then_inc(s[kind + "_rstd"], 1)
                hold(pool, s[kind + "_rstd"], r.done(g))
                pool.tensor_scalar(shift[:, i, b:b + 1], mv[:, i, b, 0:1], rstd[:, i, b:b + 1], -1.0, ALU.mult, ALU.mult
                                   ).then_inc(s[kind + "_shift"], 1)

            def score_parts(r, g):
                b = g % 4
                hold(pool, s["g_sd"], r.done(g))
                pool.tensor_copy(sd3[:, b, 0, :], sd[:, b, :]).then_inc(s["g_sd_hi"], 1)
                pool.wait_ge(s["g_sd_hi"], r.done(g))
                pool.tensor_tensor(sd_rest[:, b, 0, :], sd[:, b, :], sd3[:, b, 0, :], ALU.subtract).then_inc(s["g_rest1"], 1)
                hold(pool, s["g_rest1"], r.done(g))
                pool.tensor_copy(sd3[:, b, 1, :], sd_rest[:, b, 0, :]).then_inc(s["g_sd_mid"], 1)
                pool.wait_ge(s["g_sd_mid"], r.done(g))
                pool.tensor_tensor(sd_rest[:, b, 1, :], sd_rest[:, b, 0, :], sd3[:, b, 1, :], ALU.subtract).then_inc(s["g_rest2"], 1)
                hold(pool, s["g_rest2"], r.done(g))
                pool.tensor_copy(sd3[:, b, 2, :], sd_rest[:, b, 1, :]).then_inc(s["g_sd3"], 1)

            def step(r, k):
                if r.has(k - 6):
                    hold(pool, s["pv_norm"], r.done(k - 6))
                    pool.tensor_scalar(ey[:], y[:], 0.0, None, ALU.min).then_inc(s["y_min"], 1)
                if r.has(k - 2):
                    b = (k - 2) % SLOTS
                    pool.wait_ge(x_in[b], r.dma(k - 2))
                    pool.wait_ge(stored[b], r.dma(k - 2))
                    pool.tensor_tensor(x1[:, b, :], xin[:, b, :], vec[:, r.pair(k - 2), 0, :], ALU.add).then_inc(s["xb"], 1)
                if r.has(k - 3):
                    b = (k - 3) % SLOTS
                    pool.wait_ge(s["g_h"], r.done(k - 3))
                    pool.tensor_tensor(x1[:, b, :], x1[:, b, :], hG[:, b, :], ALU.add).then_inc(s["xf"], 1)
                if r.has(k - 6):
                    pool.wait_ge(s["y_exp"], r.done(k - 6))
                    pool.tensor_tensor(ey[:], ey[:], hG[:, (k - 6) % SLOTS, :], ALU.subtract).then_inc(s["ey_f"], 1)
                if r.has(k - 3):
                    pool.wait_ge(s["g_th"], r.done(k - 3))
                    if r.has(k - 4):
                        pool.wait_ge(s["g_sd"], r.done(k - 4))
                    for i in range(2):
                        last = pool.tensor_tensor(prod[:, i, :], th[:, (k - 3) % 2, :], vec[:, r.pair(k - 3), 2 + i, :], ALU.mult)
                    last.then_inc(s["g_prod"], 1)
                if r.has(k - 6):
                    b = (k - 6) % SLOTS
                    pool.wait_ge(s["mixed"], r.done(k - 6))
                    pool.tensor_tensor(x1[:, b, :], y[:], x1[:, b, :], ALU.add).then_inc(s["x2"], 1)
                if r.has(k + 5):
                    layernorm(r, "m", 0, k + 5)
                if r.has(k - 2):
                    layernorm(r, "g", 1, k - 2)
                if r.has(k - 3):
                    score_parts(r, k - 3)
                if r.has(k + 1):
                    g = k + 1
                    hold(pool, adj_in[g // HALF_SLOTS % 2], r.dma(g))
                    if r.has(g - 2):
                        hold(pool, s["s_biased"], r.done(g - 2))
                    pool.tensor_scalar(neg_bias[:, g % 2, :], adj8[:, g % SLOTS, :], -1.0, -NEG, ALU.add, ALU.mult
                                       ).then_inc(s["bias_mask"], 1)
                if r.has(k - 3):
                    g = k - 3
                    if r.has(g - 2):
                        hold(pool, s["z_masked"], r.done(g - 2))
                    pool.tensor_scalar(no_edge[:, g % 2, :], adj8[:, g % SLOTS, :], -1.0, 1.0, ALU.mult, ALU.add)
                    pool.tensor_scalar(floor[:, g % 2, :], adj8[:, g % SLOTS, :], LEAST, NO_EDGE, ALU.mult, ALU.add
                                       ).then_inc(s["masks"], 1)
                if r.has(k - 3):
                    hold(pool, s["g_gate"], r.done(k - 3))
                    pool.tensor_scalar(gate[:, (k - 3) % 4, :], gate[:, (k - 3) % 4, :], 0.5, 0.5, ALU.mult, ALU.add
                                       ).then_inc(s["g_sigmoid"], 1)

            def change(pair, k):
                if pair == 0 and k == 2:
                    pool.wait_ge(s["out_bias"], PAIRS)
                    pool.nop(nofuse=True)

            run_steps(pool, step, change, dma=True)

        @block.scalar
        def _(act):
            def normed(r, kind, i, g, src, dst):
                act.wait_ge(s[kind + "_shift"], r.done(g))
                act.activation(dst, src, ACT.Relu, bias=shift[:, i, g % SLOTS:g % SLOTS + 1],
                               scale=rstd[:, i, g % SLOTS:g % SLOTS + 1]).then_inc(s[kind + "_h"], 1)

            def exps(g, heads):
                for h in heads:
                    head = LA[:, g % 2, h * N:(h + 1) * N]
                    last = act.activation(head, head, ACT.Exp, bias=neg_max[:, 0, h:h + 1])
                return last

            def queries_keys(r, k, i):
                if not r.has(k + 2):
                    return
                g = k + 2 - k % 2
                c = QK_ORDER[k % 2 * 3 + i]
                q = c < KC
                pair = r.pair(g)
                act.wait_ge(s[f"qk_ps{i}"], r.done(k + 2))
                act.activation(QKT[:, c, g % 4 * N:(g % 4 + 2) * N], bank(7 if i == 2 else 6)[:, 0:2 * N], ACT.Identity,
                               bias=q_bias8[:, pair, c:c + 1] if q else cols[:, pair, c:c + 1],
                               scale=MD ** -0.5 if q else 1.0).then_inc(s[f"qk{i}"], 1)

            def step(r, k):
                if r.has(k - 1):
                    act.wait_ge(s["pt_ps"], r.done(k - 1))
                    act.activation(PTA[:].rearrange("p (e n) -> p e n", e=2), banks(3, 2)[:, :, 0:D], ACT.Copy).then_inc(s["pt"], 1)
                if r.has(k - 3):
                    act.wait_ge(s["g_hT"], r.done(k - 3))
                    act.activation(gT_hi[:], chunks(bank(7)), ACT.Copy).then_inc(s["g_hi"], 1)
                queries_keys(r, k, 0)
                if r.has(k - 5):
                    act.wait_ge(s["z_shifted"], r.done(k - 5))
                    act.activation(LG[:, (k - 5) % 2, :], LG[:, (k - 5) % 2, :], ACT.Exp).then_inc(s["z_exp"], 1)
                if r.has(k - 6):
                    act.wait_ge(s["y_min"], r.done(k - 6))
                    act.activation(ey[:], ey[:], ACT.Exp).then_inc(s["y_exp"], 1)
                if r.has(k - 3):
                    act.wait_ge(s["g_h_ps"], r.done(k - 3))
                    if r.has(k - 5):
                        act.wait_ge(s["g_prod"], r.done(k - 5))
                    act.activation(th[:, (k - 3) % 2, :], bank(7)[:, 0:D], ACT.Tanh).then_inc(s["g_th"], 1)
                if r.has(k - 2):
                    act.wait_ge(s["cT_ps"], r.done(k - 2))
                    act.activation(cT_hi[:], chunks(bank(6)), ACT.Copy).then_inc(s["cT_hi"], 1)
                if r.has(k - 5):
                    for q in range(2):
                        act.wait_ge(s[f"gpt_ps{q}"], r.done(k - 5))
                        act.activation(PTG[:, q, :], bank(3 + q), ACT.Copy).then_inc(s[f"gpt{q}"], 1)
                if r.has(k - 4):
                    act.wait_ge(s["g_sdT_ps"], r.done(k - 4))
                    act.activation(sdT[:, k % 2, :], sdT_ps, ACT.Copy).then_inc(s["g_sdT"], 1)
                if r.has(k):
                    act.wait_ge(s["s_max"], r.done(k))
                    exps(k, range(KC))
                if r.has(k - 3):
                    act.wait_ge(s["g_gate_ps"], r.done(k - 3))
                    if r.has(k - 7):
                        act.wait_ge(s["mixed"], r.done(k - 7))
                    act.activation(gate[:, (k - 3) % 4, :], bank(7)[:, 0:D], ACT.Tanh, scale=0.5).then_inc(s["g_gate"], 1)
                if r.has(k - 5):
                    act.wait_ge(s["gpt_ps2"], r.done(k - 5))
                    act.activation(PTG[:, 2, :], bank(3), ACT.Copy).then_inc(s["gpt2"], 1)
                if r.has(k + 4):
                    act.wait_ge(s["m_hT"], r.done(k + 4))
                    act.activation(hT_hi[:, :, k % 4, :], chunks(bank(7)), ACT.Copy).then_inc(s["m_hi"], 1)
                if r.has(k):
                    exps(k, range(KC, MH)).then_inc(s["s_exp"], 1)
                if r.has(k - 4):
                    act.wait_ge(s["z_ps"], r.done(k - 4))
                    act.activation(LG[:, k % 2, :].rearrange("p (e n) -> p e n", e=3), banks(0, 3),
                                   ACT.Copy, scale=SLOPE).then_inc(s["z_slope"], 1)
                if r.has(k + 2):
                    act.wait_ge(s["m_v"], r.done(k + 2))
                    act.activation(vaug[:, (k + 2) % 4, :, 0:MD], bank(7)[:, 0:D].rearrange("p (h d) -> p h d", h=MH),
                                   ACT.Copy).then_inc(s["m_vaug"], 1)
                if r.has(k - 2):
                    normed(r, "g", 1, k - 2, x1[:, (k - 2) % SLOTS, :], hG[:, (k - 2) % SLOTS, :])
                queries_keys(r, k, 1)
                queries_keys(r, k, 2)
                if r.has(k + 5):
                    normed(r, "m", 0, k + 5, xin[:, (k + 5) % SLOTS, :], hM[:])

            act.wait_ge(s["v_in"], 16 * 3 * PAIRS)
            act.activation(q_bias8[:], cols[:, :, 0:KC], ACT.Copy, scale=MD ** -0.5).then_inc(s["setup_act"], 1)
            act.wait_ge(s["setup_act"], 1)

            def change(pair, k):
                if pair:
                    for use in {-2: ("qk_ps2", "m_v"), 2: ("o_ps",), 3: ("g_gate_ps",)}[k]:
                        act.wait_ge(s[use], B)
                        act.nop(nofuse=True)
                for n in CHANGES[k]:
                    m = pair * len(PIECES) + n
                    act.wait_ge(w_in[m % 2], 16 * (m // 2 + 1))
                    act.activation(PIECES[n][1], stage[:, m % 2, :, :], ACT.Copy).then_inc(s["w_hi"], 1)

            run_steps(act, step, change)

        @block.vector
        def _(dve):
            dve.wait_ge(s["const_in"], 48)
            for i, sel in enumerate((sel_s, sel_d)):
                dve.tensor_copy(sel[:], sel_stage[:, i, :]).then_inc(s["setup_dve"], 1)
            dve.tensor_copy(idb[:], idf[:])
            dve.tensor_scalar(far_id[:], idf[:], -FAR, None, ALU.mult).then_inc(s["setup_dve"], 1)

            def statistics(r, kind, i, g, src):
                b = g % SLOTS
                dve.bn_stats(stats[:, i, b, :], src[:, b, :]).then_inc(s[kind + "_stats"], 1)
                hold(dve, s[kind + "_stats"], r.done(g))
                dve.bn_aggr(mv[:, i, b, :], stats[:, i, b, :]).then_inc(s[kind + "_mv"], 1)

            def step(r, k):
                if r.has(k - 3):
                    dve.wait_ge(s["g_hi"], r.done(k - 3))
                    dve.tensor_tensor(gT_lo[:], chunks(bank(7)), gT_hi[:].bitcast(F32), ALU.subtract).then_inc(s["g_lo"], 1)
                if r.has(k):
                    dve.wait_ge(s["s_ps"], r.done(k))
                    dve.wait_ge(s["bias_mask"], r.done(k))
                    dve.tensor_tensor(LA[:, k % 2, :].rearrange("p (e h n) -> p e h n", e=2, h=KC),
                                      banks(0, 2)[:, :, 0:D].rearrange("p e (h n) -> p e h n", h=KC),
                                      neg_bias[:, k % 2, :].unsqueeze(1).unsqueeze(1).broadcast_to([128, 2, KC, N]),
                                      ALU.add).then_inc(s["s_biased"], 1)
                c_ps = bank(5)[:, 0:MH * (MD + 1)].rearrange("p (h d) -> p h d", h=MH)
                if r.has(k - 1):
                    dve.wait_ge(s["c_ps"], r.done(k - 1))
                    dve.reciprocal(rden[:, 0, 0:MH].unsqueeze(2), c_ps[:, :, MD:MD + 1]).then_inc(s["c_rden"], 1)
                if r.has(k):
                    dve.wait_ge(s["s_biased"], r.done(k))
                    if r.has(k - 1):
                        dve.wait_ge(s["s_exp"], r.done(k - 1))
                    dve.tensor_reduce(neg_max[:, 0, 0:MH], LA[:, k % 2, :].rearrange("p (h n) -> p h n", h=MH), AX.X, ALU.max,
                                      negate=True).then_inc(s["s_max"], 1)
                if r.has(k - 1):
                    dve.wait_ge(s["c_rden"], r.done(k - 1))
                    dve.tensor_tensor(ctxn[:, (k - 1) % 2, :].rearrange("p (h d) -> p h d", h=MH), c_ps[:, :, 0:MD],
                                      rden[:, 0, 0:MH].unsqueeze(2).broadcast_to([128, MH, MD]),
                                      ALU.mult).then_inc(s["c_norm"], 1)
                if r.has(k - 3):
                    dve.wait_ge(s["g_th"], r.done(k - 3))
                    dve.tensor_tensor(haug[:, (k - 3) % 4, :, 0:GD], bank(7)[:, 0:D].rearrange("p (a e) -> p a e", a=GH),
                                      vec[:, r.pair(k - 3), 1, :].rearrange("p (a e) -> p a e", a=GH), ALU.add).then_inc(s["g_haug"], 1)
                if r.has(k - 2):
                    dve.wait_ge(s["cT_hi"], r.done(k - 2))
                    dve.tensor_tensor(cT_lo[:], chunks(bank(6)), cT_hi[:].bitcast(F32), ALU.subtract).then_inc(s["cT_lo"], 1)
                if r.has(k - 6):
                    dve.wait_ge(s["ey_f"], r.done(k - 6))
                    dve.scalar_tensor_tensor(y[:], y[:], 0.0, ey[:], ALU.max, ALU.add).then_inc(s["elu_f"], 1)
                if r.has(k + 5):
                    g = k + 5
                    b = g % SLOTS
                    dve.wait_ge(x_in[b], r.dma(g))
                    dve.bn_stats(stats[:, 0, b, :], xin[:, b, :]).then_inc(s["m_stats"], 1)
                if r.has(k - 6):
                    dve.wait_ge(s["elu_f"], r.done(k - 6))
                    dve.wait_ge(s["g_sigmoid"], r.done(k - 6))
                    dve.scalar_tensor_tensor(y[:], y[:], -1.0, gate[:, (k - 6) % 4, :], ALU.add, ALU.mult).then_inc(s["mixed"], 1)
                if r.has(k + 5):
                    hold(dve, s["m_stats"], r.done(g))
                    dve.bn_aggr(mv[:, 0, b, :], stats[:, 0, b, :]).then_inc(s["m_mv"], 1)
                if r.has(k - 3):
                    dve.wait_ge(s["g_prod"], r.done(k - 3))
                    dve.tensor_reduce(sd[:, (k - 3) % 4, :], prod[:].rearrange("p k (a e) -> p (k a) e", a=GH), AX.X,
                                      ALU.add).then_inc(s["g_sd"], 1)
                if r.has(k - 2):
                    g = k - 2
                    b = g % SLOTS
                    dve.wait_ge(s["o_ps"], r.done(g))
                    dve.wait_ge(s["xb"], r.done(g))
                    dve.tensor_tensor(x1[:, b, :], bank(6)[:, 0:D], x1[:, b, :], ALU.add).then_inc(s["x1"], 1)
                    dve.wait_ge(s["x1"], r.done(g))
                    dve.bn_stats(stats[:, 1, b, :], x1[:, b, :]).then_inc(s["g_stats"], 1)
                if r.has(k + 4):
                    dve.wait_ge(s["m_hi"], r.done(k + 4))
                    dve.tensor_tensor(hT_lo[:, :, k % 4, :], chunks(bank(7)), hT_hi[:, :, k % 4, :].bitcast(F32),
                                      ALU.subtract).then_inc(s["m_lo"], 1)
                if r.has(k - 2):
                    hold(dve, s["g_stats"], r.done(g))
                    dve.bn_aggr(mv[:, 1, b, :], stats[:, 1, b, :]).then_inc(s["g_mv"], 1)
                if r.has(k - 4):
                    Lk = LG[:, k % 2, :].rearrange("p (a n) -> p a n", a=GH)
                    L3 = LG[:, k % 2, :].rearrange("p (e n) -> p e n", e=3)
                    dve.wait_ge(s["z_slope"], r.done(k - 4))
                    dve.tensor_tensor(L3, banks(0, 3), L3, ALU.max).then_inc(s["z_leaky"], 1)
                    dve.wait_ge(s["z_leaky"], r.done(k - 4))
                    dve.wait_ge(s["masks"], r.done(k - 4))
                    dve.tensor_tensor(Lk, Lk, floor[:, k % 2, :].unsqueeze(1).broadcast_to([128, GH, N]),
                                      ALU.max).then_inc(s["z_masked"], 1)
                pv = bank(5)[:, 0:GH * (GD + 1)].rearrange("p (a e) -> p a e", a=GH)
                if r.has(k - 5):
                    dve.wait_ge(s["pv_ps"], r.done(k - 5))
                    dve.reciprocal(rden[:, 1, :].unsqueeze(2), pv[:, :, GD:GD + 1]).then_inc(s["pv_rden"], 1)
                if r.has(k - 4):
                    dve.wait_ge(s["z_masked"], r.done(k - 4))
                    dve.tensor_reduce(neg_max[:, 1, :], Lk, AX.X, ALU.max, negate=True).then_inc(s["z_max"], 1)
                if r.has(k - 5):
                    dve.wait_ge(s["pv_rden"], r.done(k - 5))
                    if r.has(k - 6):
                        dve.wait_ge(s["x2"], r.done(k - 6))
                    dve.tensor_tensor(y[:].rearrange("p (a e) -> p a e", a=GH), pv[:, :, 0:GD],
                                      rden[:, 1, :].unsqueeze(2).broadcast_to([128, GH, GD]),
                                      ALU.mult).then_inc(s["pv_norm"], 1)
                if r.has(k - 4):
                    dve.wait_ge(s["z_max"], r.done(k - 4))
                    dve.tensor_tensor(Lk, Lk, neg_max[:, 1, :].unsqueeze(2).broadcast_to([128, GH, N]),
                                      ALU.add).then_inc(s["z_shifted"], 1)

            dve.wait_ge(s["v_in"], 16 * 3 * PAIRS)
            for pair in range(PAIRS):
                dve.tensor_copy(bv_cols[pair], cols[:, pair, 2 * KC:3 * KC].unsqueeze(2).broadcast_to([128, KC, 128])
                                ).then_inc(s["bv_cols"], 1)
            for pair in range(PAIRS):
                row = hb_row[:, pair, :]
                at = 7 * pair
                dve.tensor_copy(hb_part[:, 0, :], row).then_inc(s["hb_step"], 1)
                dve.wait_ge(s["hb_step"], at + 1)
                dve.tensor_tensor(hb_rest, row, hb_part[:, 0, :], ALU.subtract).then_inc(s["hb_step"], 1)
                dve.wait_ge(s["hb_step"], at + 2)
                dve.tensor_copy(hb_part[:, 1, :], hb_rest).then_inc(s["hb_step"], 1)
                dve.wait_ge(s["hb_step"], at + 3)
                dve.tensor_tensor(hb_rest, hb_rest, hb_part[:, 1, :], ALU.subtract).then_inc(s["hb_step"], 1)
                dve.wait_ge(s["hb_step"], at + 4)
                dve.tensor_copy(hb_part[:, 2, :], hb_rest)
                dve.tensor_scalar(hb_acc, hb_part[:, 0, :], idf[0:PARTS, 0:1], None, ALU.mult).then_inc(s["hb_step"], 1)
                dve.wait_ge(s["hb_step"], at + 5)
                dve.scalar_tensor_tensor(hb_acc, hb_part[:, 1, :], idf[0:PARTS, 1:2], hb_acc, ALU.mult, ALU.add).then_inc(s["hb_step"], 1)
                dve.wait_ge(s["hb_step"], at + 6)
                dve.scalar_tensor_tensor(hb3[:, pair, :], hb_part[:, 2, :], idf[0:PARTS, 2:3], hb_acc, ALU.mult, ALU.add
                                         ).then_inc(s["hb_step"], 1)
                dve.wait_ge(s["hb_step"], at + 7)

            def change(pair, k):
                for n in CHANGES[k]:
                    w, hi, lo, at = PIECES[n]
                    dve.wait_ge(s["w_hi"], pair * len(PIECES) + n + 1)
                    dve.tensor_tensor(lo, stage[:, n % 2, :, :], hi.bitcast(F32), ALU.subtract).then_inc(s["w_split"], 1)
                if pair == 0 and k == -2:
                    for i in range(PAIRS):
                        dve.wait_ge(s["out_bias_ps"], i + 1)
                        dve.tensor_tensor(vec[:, i, 0, :], bank(i)[:, 0:D], vec[:, i, 0, :], ALU.add).then_inc(s["out_bias"], 1)

            run_steps(dve, step, change, dma=True)

        @block.tensor
        def _(pe):
            pe.wait_ge(s["setup_dve"], 3)
            pe.wait_ge(s["setup_pool"], 1)

            def features(src, dst):
                for c in range(KC):
                    last = pe.transpose(dst[:, c * 128:(c + 1) * 128], src[:, c * 128:(c + 1) * 128], idf[:])
                return last

            def nodes_times(dst, hi, lo, w_hi, w_lo, at, begun=False):
                n = 0
                for a, w in ((hi, w_hi), (hi, w_lo), (lo, w_hi)):
                    for c in range(KC):
                        last = pe.matmul(dst, a(c), w[:, c, at:at + D], start=(n == 0 and not begun), stop=(n == 3 * KC - 1))
                        n += 1
                return last

            def queries_keys(r, k, i, *bank_users):
                if not r.has(k + 2):
                    return
                g = k + 2 - k % 2
                c = QK_ORDER[k % 2 * 3 + i]
                if i == 0:
                    pe.wait_ge(s["m_lo"], r.done(g + 1))
                wait_latest(pe, r, *bank_users)
                dst = bank(7 if i == 2 else 6)[:, 0:2 * N]
                m = 0
                for w, a in ((qk_hi, hT_hi), (qk_lo, hT_hi), (qk_hi, hT_lo)):
                    for j in range(KC):
                        last = pe.matmul(dst, w[:, j, c * 128:(c + 1) * 128],
                                         a[:, j, g % 4:g % 4 + 2, :].rearrange("p b n -> p (b n)"), start=(m == 0), stop=(m == 3 * KC - 1))
                        m += 1
                last.then_inc(s[f"qk_ps{i}"], 1)

            def graph_transposes(r, g, q):
                for a in range(4 * q, 4 * q + 4):
                    last = pe.transpose(bank(3 + q % 2)[:, (a % 4) * N:(a % 4 + 1) * N], LG[:, g % 2, a * N:(a + 1) * N], idf[:])
                last.then_inc(s[f"gpt_ps{q}"], 1)

            def step(r, k):
                if r.has(k - 1):
                    pe.wait_ge(s["s_exp"], r.done(k - 1))
                    wait_latest(pe, r, ("gpt2", k - 6), ("pt", k - 2))
                    for i in range(MH):
                        last = pe.transpose(bank(3 + i // KC)[:, (i % KC) * N:(i % KC + 1) * N],
                                            LA[:, (k - 1) % 2, i * N:(i + 1) * N], idf[:])
                    last.then_inc(s["pt_ps"], 1)
                if r.has(k):
                    if k % 2 == 0:
                        for i in range(3):
                            pe.wait_ge(s[f"qk{i}"], r.done(k + 1))
                    wait_latest(pe, r, ("z_leaky", k - 5), ("s_biased", k - 1))
                    for i in range(MH):
                        h = head_of(i)
                        rows = slice(64 * (h % 2), 64 * (h % 2) + 64)
                        at = slice(k % 4 * N, (k % 4 + 1) * N)
                        last = pe.matmul(bank(i // KC)[:, (i % KC) * N:(i % KC + 1) * N],
                                         QKT[rows, h // 2, at], QKT[rows, KC + h // 2, at], start=True, stop=True)
                    last.then_inc(s["s_ps"], 1)
                if r.has(k - 3):
                    pe.wait_ge(s["g_h"], r.done(k - 3))
                    wait_latest(pe, r, ("qk2", k + 1), ("g_gate", k - 4))
                    features(hG[:, (k - 3) % SLOTS, :], bank(7)).then_inc(s["g_hT"], 1)
                queries_keys(r, k, 0, ("qk1", k + 1))
                if r.has(k - 1):
                    pe.wait_ge(s["pt"], r.done(k - 1))
                    pe.wait_ge(s["m_vaug"], r.done(k - 1))
                    wait_latest(pe, r, ("pv_norm", k - 6), ("g_sdT", k - 5), ("c_norm", k - 2))
                    for i in range(MH):
                        h = head_of(i)
                        last = pe.matmul(bank(5)[:, h * (MD + 1):(h + 1) * (MD + 1)], PTA[:, i * N:(i + 1) * N],
                                         vaug[:, (k - 1) % 4, h, :], start=True, stop=True)
                    last.then_inc(s["c_ps"], 1)
                g_hi, g_lo = (lambda c: gT_hi[:, c, :]), (lambda c: gT_lo[:, c, :])
                if r.has(k - 3):
                    pe.wait_ge(s["g_lo"], r.done(k - 3))
                    nodes_times(bank(7)[:, 0:D], g_hi, g_lo, hg_hi, hg_lo, 0).then_inc(s["g_h_ps"], 1)
                if r.has(k - 2):
                    pe.wait_ge(s["c_norm"], r.done(k - 2))
                    wait_latest(pe, r, ("qk0", k + 2), ("x1", k - 3))
                    features(ctxn[:, k % 2, :], bank(6)).then_inc(s["cT_ps"], 1)
                if r.has(k - 5):
                    pe.wait_ge(s["z_exp"], r.done(k - 5))
                    wait_latest(pe, r, ("pt", k - 1), ("gpt2", k - 6))
                    graph_transposes(r, k - 5, 0)
                    graph_transposes(r, k - 5, 1)
                if r.has(k - 4):
                    pe.wait_ge(s["g_sd3"], r.done(k - 4))
                    wait_latest(pe, r, ("c_norm", k - 1), ("pv_norm", k - 6), ("g_sdT", k - 5))
                    pe.transpose(sdT_ps, sd3[:, k % 4, :, :].rearrange("p a n -> p (a n)"), idb[:]).then_inc(s["g_sdT_ps"], 1)
                if r.has(k - 3):
                    pe.wait_ge(s["g_haug"], r.done(k - 3))
                    pe.matmul(bank(7)[:, 0:D], ones3[:], hb3[:, r.pair(k - 3), :], start=True, stop=False)
                    nodes_times(bank(7)[:, 0:D], g_hi, g_lo, hg_hi, hg_lo, D, begun=True).then_inc(s["g_gate_ps"], 1)
                if r.has(k - 5):
                    pe.wait_ge(s["gpt0"], r.done(k - 5))
                    graph_transposes(r, k - 5, 2)
                if r.has(k - 2):
                    pe.wait_ge(s["cT_lo"], r.done(k - 2))
                    nodes_times(bank(6)[:, 0:D], lambda c: cT_hi[:, c, :], lambda c: cT_lo[:, c, :], vf_hi, vf_lo, D
                                ).then_inc(s["o_ps"], 1)
                if r.has(k + 4):
                    pe.wait_ge(s["m_h"], r.done(k + 4))
                    wait_latest(pe, r, ("g_gate", k - 3), ("qk2", k + 1), ("m_lo", k + 3))
                    features(hM, bank(7)).then_inc(s["m_hT"], 1)
                if r.has(k - 4):
                    pe.wait_ge(s["masks"], r.done(k - 4))
                    pe.wait_ge(s["g_sdT"], r.done(k - 4))
                    wait_latest(pe, r, ("s_biased", k), ("z_leaky", k - 5))
                    for q in range(QUADS):
                        four = bank(q).rearrange("p (a n) -> p a n", a=4)
                        pe.matmul(four, sdT[:, k % 2, :], sel_s[:, 4 * q:4 * q + 4].unsqueeze(2).broadcast_to([PARTS * SD, 4, N]), start=True, stop=False)
                        for a in range(4):
                            pe.matmul(four[:, a, :], sel_d[:, 4 * q + a:4 * q + a + 1].broadcast_to([PARTS * SD, 128]), sdT[:, k % 2, :], start=False, stop=False)
                        last = pe.matmul(four, far_id[:], no_edge[:, k % 2, :].unsqueeze(1).broadcast_to([128, 4, N]),
                                         start=False, stop=True)
                    last.then_inc(s["z_ps"], 1)
                if r.has(k + 2):
                    wait_latest(pe, r, ("m_lo", k + 4), ("g_gate", k - 3))
                    b = (k + 2) % 4
                    nodes_times(bank(7)[:, 0:D], lambda c: hT_hi[:, c, b, :], lambda c: hT_lo[:, c, b, :], vf_hi, vf_lo, 0
                                ).then_inc(s["m_v"], 1)
                if r.has(k - 5):
                    wait_latest(pe, r, ("g_sdT", k - 4), ("pv_norm", k - 6))
                    for q in range(QUADS):
                        pe.wait_ge(s[f"gpt{q}"], r.done(k - 5))
                        for a in range(4 * q, 4 * q + 4):
                            last = pe.matmul(bank(5)[:, a * (GD + 1):(a + 1) * (GD + 1)], PTG[:, q, (a % 4) * N:(a % 4 + 1) * N],
                                             haug[:, (k - 5) % 4, a, :], start=True, stop=True)
                    last.then_inc(s["pv_ps"], 1)
                queries_keys(r, k, 1, ("x1", k - 2), ("qk0", k + 2))
                queries_keys(r, k, 2, ("m_vaug", k + 2))

            def change(pair, k):
                if pair == 0 and k == -2:
                    pe.wait_ge(s["wf_in"], 16 * PAIRS)
                    pe.wait_ge(s["bv_cols"], PAIRS)
                    for i in range(PAIRS):
                        for c in range(KC):
                            last = pe.matmul(bank(i)[:, 0:D], bv_cols[i][:, c, :], wf_stage[i][:, c, :], start=(c == 0), stop=(c == KC - 1))
                        last.then_inc(s["out_bias_ps"], 1)
                if pair == 0 and k == 2:
                    pe.wait_ge(s["hb_step"], 7 * PAIRS)
                    pe.nop(nofuse=True)
                pe.wait_ge(s["w_split"], split_count(pair, k))
                pe.nop(nofuse=True)

            run_steps(pe, step, change)


def kernel(**inputs):
    import numpy as np
    import concourse.bacc as bacc
    from concourse.bass_utils import run_bass_kernel_spmd as run

    def of(layer, name):
        return np.asarray(inputs[f"L{layer}_gnn_{name}"])

    w_qk = np.stack([np.concatenate([of(m, "Wq"), of(m, "Wk")], 1) for m in (0, 2)])
    w_vf = np.stack([np.concatenate([of(m, "Wv"), of(m, "Wf")], 1) for m in (0, 2)])
    w_hg = np.stack([np.concatenate([of(g, "W").transpose(1, 0, 2).reshape(D, D), of(g, "H_w").T], 1) for g in (1, 3)])
    b_cols = np.stack([np.concatenate([of(m, "bq"), of(m, "bk"), of(m, "bv")]).reshape(3 * KC, 128).T for m in (0, 2)])
    vecs = np.stack([np.stack([of(g - 1, "bf"), np.tile(of(g, "b"), GH),
                               of(g, "w_src").reshape(D), of(g, "w_dst").reshape(D)]) for g in (1, 3)])
    h_b = np.stack([of(g, "H_b") for g in (1, 3)])
    row = np.arange(PARTS * SD)[:, None]
    head = np.arange(GH)[None, :]
    sel_src = (row % SD == head).astype(np.float32)
    sel_dst = (row % SD == GH + head).astype(np.float32)
    arrays = {
        "x": np.asarray(inputs["x"]), "adj": np.asarray(inputs["adj"]), "w_qk": w_qk, "w_vf": w_vf, "w_hg": w_hg,
        "b_cols": b_cols, "vecs": vecs, "h_b": h_b, "ident": np.eye(128, dtype=np.float32), "sel_src": sel_src, "sel_dst": sel_dst,
    }
    nc = bacc.Bacc("TRN2", target_bir_lowering=False, num_devices=1)
    args = []
    for name, a in arrays.items():
        arrays[name] = a = np.ascontiguousarray(a)
        args.append(nc.dram_tensor(name, a.shape, mybir.dt.from_np(a.dtype), kind="ExternalInput").ap())
    args.append(nc.dram_tensor("out", inputs["x"].shape, F32, kind="ExternalOutput").ap())
    graph_stack(nc, *args)
    r = run(nc, [arrays], core_ids=[0])
    return r.results[0]["out"]
```
